# Optimizing a Trainium2 kernel written in Bass

```python
import numpy as np
import jax
import jax.numpy as jnp

def _softmax(x, axis=-1):
    return jax.nn.softmax(x, axis=axis)

def _gelu(x):
    return jax.nn.gelu(x, approximate=True)

def _silu(x):
    return jax.nn.silu(x)

def _sigmoid(x):
    return jax.nn.sigmoid(x)

def _layernorm(x, axis=-1, eps=1e-05):
    m = jnp.mean(x, axis=axis, keepdims=True)
    v = jnp.var(x, axis=axis, keepdims=True)
    return (x - m) / jnp.sqrt(v + eps)

def _scatter_add(tgt, idx, src, axis=0):
    return tgt.at[idx].add(src)

def _segment_sum(src, seg, n):
    return jax.ops.segment_sum(src, seg, n)
kernel_name = 'mk_adj_resnorm_d4_adj_r2_e9cf9f'

def setup_inputs(seed: int=0):
    np.random.seed(seed)
    _w = jnp.asarray

    def _rec_inputs():
        import jax
        import jax.numpy as jnp
        _gk = jax.random.key(seed)
        x = -0.000929 + 1 * jax.random.normal(jax.random.fold_in(_gk, 1), (4096, 128), jnp.float32)
        _a = jax.random.bernoulli(jax.random.fold_in(_gk, 2), 0.000976562, (4096, 4096))
        _a = jnp.logical_or(_a, jnp.eye(4096, dtype=bool))
        _af = _a.astype(jnp.float32)
        adj = _af
        return (x, adj)
    x, adj = _rec_inputs()

    def _L0_gnn_setup():
        import jax, jax.numpy as jnp
        import numpy as np
        N = 4096
        DIN = 128
        F = 64
        H = 2
        NEG_BIG = -10000000000.0
        key = jax.random.key(seed)
        k1, k2, k3, k4 = jax.random.split(key, 4)
        x = jax.random.normal(k1, (N, DIN), dtype=jnp.float32)
        adj = (jax.random.uniform(k2, (N, N)) < 0.002).astype(jnp.float32)
        idx = jnp.arange(N)
        adj = adj.at[idx, idx].set(1.0)
        kernels = jax.random.normal(k3, (H, DIN, F), dtype=jnp.float32) * 0.05
        att_kernels = jax.random.normal(k4, (H, 2 * F), dtype=jnp.float32) * 0.05
        return {'x': x, 'adj': adj, 'kernels': kernels, 'att_kernels': att_kernels}
    _L0_gnn_all = _L0_gnn_setup()
    _L0_gnn_in = {k: v for k, v in _L0_gnn_all.items() if k in ('kernels', 'att_kernels')}
    del _L0_gnn_all

    def _L1_gnn_setup():
        import jax, jax.numpy as jnp
        import numpy as np
        N, E, D = (4096, 4096, 128)
        key = jax.random.key(seed)
        k1, k2 = jax.random.split(key)
        X = jax.random.normal(k1, (N, D), dtype=jnp.float32)
        H = jax.random.uniform(k2, (N, E), dtype=jnp.float32)
        return {'X': X, 'H': H}
    _L1_gnn_all = _L1_gnn_setup()
    _L1_gnn_in = {k: v for k, v in _L1_gnn_all.items() if k in ()}
    del _L1_gnn_all

    def _L2_gnn_setup():
        import jax, jax.numpy as jnp
        import numpy as np
        N = 8192
        F_IN = 128
        F_OUT = 128
        key = jax.random.key(seed)
        k1, k2, k3 = jax.random.split(key, 3)
        inp = jax.random.normal(k1, (N, F_IN), dtype=jnp.float32)
        adj = jax.random.uniform(k2, (N, N), dtype=jnp.float32)
        stdv = 1.0 / np.sqrt(F_OUT)
        weight = jax.random.uniform(k3, (F_IN * 2, F_OUT), dtype=jnp.float32, minval=-stdv, maxval=stdv)
        return {'input': inp, 'adj': adj, 'weight': weight}
    _L2_gnn_all = _L2_gnn_setup()
    _L2_gnn_in = {k: v for k, v in _L2_gnn_all.items() if k in ('weight',)}
    del _L2_gnn_all

    def _L3_gnn_setup():
        import jax, jax.numpy as jnp
        import numpy as np
        EPS = 1e-06
        PN_SCALE = 1.0

        def pair_norm(x):
            x = x - jnp.mean(x, axis=0, keepdims=True)
            rownorm_mean = jnp.sqrt(jnp.mean(jnp.sum(x * x, axis=1) + EPS))
            return PN_SCALE * x / rownorm_mean
        key = jax.random.key(seed)
        k1, k2, k3, k4 = jax.random.split(key, 4)
        N, IN, OUT = (8192, 128, 128)
        x = jax.random.normal(k1, (N, IN), dtype=jnp.float32)
        adj = jax.random.uniform(k2, (N, N), dtype=jnp.float32)
        bound = float(np.sqrt(6.0 / (IN + OUT)))
        weight = jax.random.uniform(k3, (IN, OUT), dtype=jnp.float32, minval=-bound, maxval=bound)
        self_weight = jax.random.uniform(k4, (IN, OUT), dtype=jnp.float32, minval=-bound, maxval=bound)
        return {'x': x, 'adj': adj, 'weight': weight, 'self_weight': self_weight}
    _L3_gnn_all = _L3_gnn_setup()
    _L3_gnn_in = {k: v for k, v in _L3_gnn_all.items() if k in ('weight', 'self_weight')}
    del _L3_gnn_all
    return {'x': x, 'adj': adj, 'L0_gnn_kernels': _L0_gnn_in['kernels'], 'L0_gnn_att_kernels': _L0_gnn_in['att_kernels'], 'L2_gnn_weight': _L2_gnn_in['weight'], 'L3_gnn_weight': _L3_gnn_in['weight'], 'L3_gnn_self_weight': _L3_gnn_in['self_weight']}

def reference(x, adj, L0_gnn_kernels, L0_gnn_att_kernels, L2_gnn_weight, L3_gnn_weight, L3_gnn_self_weight):
    import jax
    import jax.numpy as jnp

    def _L0_gnn_ref(x, adj, kernels, att_kernels):
        import jax, jax.numpy as jnp
        import numpy as np
        N = 4096
        DIN = 128
        F = 64
        H = 2
        NEG_BIG = -10000000000.0
        conv = jnp.einsum('nd,hdf->hnf', x, kernels)
        a_self = jnp.einsum('hnf,hf->hn', conv, att_kernels[:, :F])
        a_neigh = jnp.einsum('hnf,hf->hn', conv, att_kernels[:, F:])
        scores = jax.nn.elu(a_self[:, :, None] + a_neigh[:, None, :], alpha=1.0)
        mask = jnp.exp(adj * NEG_BIG) * NEG_BIG
        p = jax.nn.softmax(scores + mask[None, :, :], axis=-1)
        out = jnp.einsum('hnm,hmf->hnf', p, conv)
        return out.transpose(1, 0, 2).reshape(N, H * F)

    def _L1_gnn_ref(X, H):
        import jax, jax.numpy as jnp
        import numpy as np
        N, E, D = (4096, 4096, 128)
        msg = jnp.matmul(H.T, X)
        inv_deg = 1.0 / H.sum(axis=0)
        inv_deg = jnp.where(jnp.isinf(inv_deg), 0.0, inv_deg)
        return msg * inv_deg[:, None]

    def _L2_gnn_ref(input, adj, weight):
        import jax, jax.numpy as jnp
        import numpy as np
        N = 8192
        F_IN = 128
        F_OUT = 128
        support = jnp.matmul(adj, input)
        w_self, w_agg = (weight[:F_IN], weight[F_IN:])
        return jnp.matmul(input, w_self) + jnp.matmul(support, w_agg)

    def _L3_gnn_ref(x, adj, weight, self_weight):
        import jax, jax.numpy as jnp
        import numpy as np
        EPS = 1e-06
        PN_SCALE = 1.0

        def pair_norm(x):
            x = x - jnp.mean(x, axis=0, keepdims=True)
            rownorm_mean = jnp.sqrt(jnp.mean(jnp.sum(x * x, axis=1) + EPS))
            return PN_SCALE * x / rownorm_mean
        support = x @ weight
        output = support + adj @ support
        output = output + x @ self_weight
        output = jax.nn.relu(output)
        return pair_norm(output)
    x = _layernorm(x + _L0_gnn_ref(x, adj, L0_gnn_kernels, L0_gnn_att_kernels), axis=-1)
    x = _layernorm(x + _L1_gnn_ref(x, adj), axis=-1)
    x = _layernorm(x + _L2_gnn_ref(x, adj, L2_gnn_weight), axis=-1)
    x = _layernorm(x + _L3_gnn_ref(x, adj, L3_gnn_weight, L3_gnn_self_weight), axis=-1)
    return x

_drawn_inputs = setup_inputs


def setup_inputs(seed=0):
    import zlib

    import numpy as np

    out = dict(_drawn_inputs(seed))
    spreads = {}
    factors = {}
    for name, (base, spread) in spreads.items():
        noise = np.random.default_rng([zlib.crc32(name.encode()), seed]).standard_normal(out[name].shape)
        drawn = base * np.exp(spread * noise) if base else spread * noise
        out[name] = jnp.asarray(drawn.astype(out[name].dtype))
    for name, factor in factors.items():
        out[name] = (out[name] * factor).astype(out[name].dtype)
    return out
```

```python
from contextlib import ExitStack

import concourse.bass as bass
from concourse import mybir


def build(nc, x, adj, att_w, att_v, w2, w3, w3_self, out):
    fp32, fp16, bf16, fp8 = mybir.dt.float32, mybir.dt.float16, mybir.dt.bfloat16, mybir.dt.float8e4
    int32 = mybir.dt.int32
    ALU, ACT, AX = mybir.AluOpType, mybir.ActivationFunctionType, mybir.AxisListType

    P = 128
    N, D = x.shape
    HEADS, _, F = att_w.shape
    NT = N // P
    GT = 4
    GW = GT * P
    NG = NT // GT
    PAIRS = NT // 2
    LOADS = 4
    LW = N // LOADS
    PPL = PAIRS // LOADS
    XB, EB = 4, 4
    FX = F + 1
    BIG = float(2 ** 100)
    MASKED = 127.0
    TOP = 60.0
    HL = 1024.0
    EPS = 1e-5
    NEWTON = 3
    LN_LINKS = 5 + 3 * NEWTON
    PAIR_EPS = 1e-6

    adj8 = nc.dram_tensor("adj8", [NG, P, NT, GW // 4], fp32, kind="Internal").ap()
    adjT8 = nc.dram_tensor("adjT8", [NG, P, NT, GW // 4], fp32, kind="Internal").ap()
    ea_dram = nc.dram_tensor("ea_dram", [HEADS * NT, P], fp32, kind="Internal").ap()

    ctx = ExitStack()
    with ctx:
        def sb(name, shape, dt=fp32):
            return ctx.enter_context(nc.sbuf_tensor(name, shape, dt))

        def sem(name):
            return ctx.enter_context(nc.semaphore(name))

        xn = sb("xn", [P, NT, D])
        parts_a = sb("parts_a", [P, NT, 2 * D + 1], fp16)
        convx = sb("convx", [P, NT, HEADS, FX])
        ea_row = sb("ea_row", [P, HEADS, N])
        nat = sb("nat", [P, LOADS, GT, LW], fp8)
        stage8 = sb("stage8", [P, 2, 2 * PPL, GW], fp8)
        xring = sb("xring", [P, XB, 2, HEADS, GW])
        ering = sb("ering", [P, EB, 2, HEADS, GW])
        oT = sb("oT", [FX, HEADS, GW])
        stream = xring[:].rearrange("p a b h n -> p (a b h n)").bitcast(fp8).rearrange(
            "p (s t n) -> p s t n", s=2, t=NT)
        stream32 = xring[:].rearrange("p a b h n -> p (a b h n)").rearrange("p (s t n) -> p s t n", s=2, t=NT)
        parts_b = ea_row[:, 0, :].bitcast(fp16).rearrange("p (t d) -> p t d", t=NT)
        act3 = ea_row[:, 1, :].rearrange("p (t d) -> p t d", t=NT)
        eflat = ering[:].rearrange("p a b h n -> p (a b h n)")
        xs = eflat[:, 0:2 * GW].rearrange("p (s n) -> p s n", s=2)
        xT = eflat[:, 2 * GW:4 * GW].rearrange("p (s n) -> p s n", s=2)
        sT = eflat[:, 4 * GW:6 * GW].rearrange("p (s n) -> p s n", s=2)
        tmp = eflat[:, 6 * GW:8 * GW].rearrange("p (s t d) -> p s t d", s=2, t=GT)
        msg = eflat[:, 8 * GW:10 * GW].rearrange("p (s t d) -> p s t d", s=2, t=GT)
        sq_junk = eflat[:, 8 * GW:(8 + NG) * GW].rearrange("p (s n) -> p s n", s=NG)

        kc = sb("kc", [P, HEADS, F])
        att_b = sb("att_b", [P, HEADS, 2, F])
        vprod = sb("vprod", [P, HEADS, 2, F])
        rhs_a = sb("rhs_a", [P, 2 * F + 4])
        ab = sb("ab", [P, NT, 4])
        m4 = sb("m4", [P, 4])
        top4 = sb("top4", [P, 4])
        guard = sb("guard", [P, 12])
        ea_n = sb("ea_n", [P, HEADS, NT])
        eaT = sb("eaT", [HEADS * NT, P])
        eb = sb("eb", [P, NT, HEADS])
        ident_f = sb("ident_f", [P, P])
        ident_big = sb("ident_big", [P, P], bf16)
        minus_w = sb("minus_w", [P, P], bf16)
        ones_m = sb("ones_m", [P, GW], bf16)
        ones_f = sb("ones_f", [P, P])
        st = sb("st", [P, GT, 6])
        mv = sb("mv", [P, GT, 2])
        rstd = sb("rstd", [P, GT])
        var = sb("var", [P, 2 * GT])
        rden = sb("rden", [P, HEADS, GT])
        deg = sb("deg", [P, 4, GT])
        w2s = sb("w2s", [P, 2, D])
        w3s = sb("w3s", [P, 2, D])
        mean_c = sb("mean_c", [P, D])
        sq = sb("sq", [P, NG])
        pn = sb("pn", [P, 4])

        ps = ctx.enter_context(nc.psum_tensor("ps", [P, 8, GW], fp32))

        passed = sem("passed")
        x_loaded = [sem(f"x_loaded{i}") for i in range(4)]
        w_loaded = sem("w_loaded")
        w23_loaded = sem("w23_loaded")
        ident_step = sem("ident_step")
        ident_ready = sem("ident_ready")
        consts_ready = sem("consts_ready")
        v_ready = sem("v_ready")
        pro_chain = sem("pro_chain")
        xT_made = sem("xT_made")
        xT_copied = sem("xT_copied")
        conv_made = sem("conv_made")
        conv_copied = sem("conv_copied")
        m4_ready = sem("m4_ready")
        top4_ready = sem("top4_ready")
        guard_ready = sem("guard_ready")
        eb_ready = sem("eb_ready")
        exps_ready = sem("exps_ready")
        eaT_made = sem("eaT_made")
        eaT_copied = sem("eaT_copied")
        ea_saved = sem("ea_saved")
        ea_loaded = sem("ea_loaded")
        nat_loaded = [sem(f"nat_loaded{i}") for i in range(LOADS)]
        nat_saved = [sem(f"nat_saved{i}") for i in range(LOADS)]
        mask_made = sem("mask_made")
        mask_kept = sem("mask_kept")
        stage_saved = [sem(f"stage_saved{i}") for i in range(2)]
        t_made = sem("t_made")
        e_made = sem("e_made")
        p_made = sem("p_made")
        pv_done = sem("pv_done")
        acc_copied = sem("acc_copied")
        back_made = sem("back_made")
        att_chain = sem("att_chain")
        parts1_ready = sem("parts1_ready")
        l1_loaded = [sem(f"l1_loaded{i}") for i in range(2)]
        l1_summed = sem("l1_summed")
        l1_low = sem("l1_low")
        l1_taken = sem("l1_taken")
        l1_chain = sem("l1_chain")
        parts2_ready = sem("parts2_ready")
        names = ("loaded0", "loaded1", "summed", "staged", "xT_made", "xT_copied", "sT_copied",
                 "product", "taken", "chain", "parts_out", "colsum")
        agg = [{k: sem(f"l{n}_{k}") for k in names} for n in (2, 3)]
        w3_ready = sem("w3_ready")
        end_chain = sem("end_chain")
        squares = sem("squares")
        total_made = sem("total_made")
        mean_copied = sem("mean_copied")
        out_ready = sem("out_ready")
        out_saved = sem("out_saved")

        block = ctx.enter_context(nc.Block())

        @block.sync
        def _(sp):
            x_v = x.rearrange("(t p) d -> p t d", p=P)
            for i in range(4):
                sp.dma_start(xn[:, i * NT // 4:(i + 1) * NT // 4, :],
                             x_v[:, i * NT // 4:(i + 1) * NT // 4, :]).then_inc(x_loaded[i], 16)
            sp.dma_start(w2s[:], w2.rearrange("(a d) n -> d a n", a=2)).then_inc(w23_loaded, 16)
            sp.dma_start(w3s[:, 0, :], w3_self).then_inc(w23_loaded, 16)
            sp.dma_start(w3s[:, 1, :], w3).then_inc(w23_loaded, 16)

            sp.wait_ge(eaT_copied, 1)
            sp.dma_start(ea_dram, eaT[:]).then_inc(ea_saved, 16)
            sp.wait_ge(ea_saved, 16)
            sp.dma_start(ea_row[:].rearrange("p h n -> p (h n)"),
                         ea_dram.rearrange("t p -> (t p)").partition_broadcast(P)).then_inc(ea_loaded, 16)

            with sp.Fori(0, NG) as g:
                for k in range(LOADS):
                    sp.wait_ge(nat_loaded[k], (g + 1) * 16)
                    for half in range(2):
                        c = 2 * k + half
                        sp.dma_start(adj8[c, :, bass.ds(g * GT, GT), :],
                                     nat[:, k, :, half * GW:(half + 1) * GW].bitcast(fp32)
                                     ).then_inc(nat_saved[k], 16)
                    sp.wait_ge(mask_kept, g * PAIRS + (k + 1) * PPL)
                    sp.dma_start(adjT8[bass.ds(g, 1), :, 2 * PPL * k:2 * PPL * (k + 1), :]
                                 .rearrange("a p t n -> p (a t n)"),
                                 stage8[:, k % 2, :, :].rearrange("p t n -> p (t n)").bitcast(fp32)
                                 ).then_inc(stage_saved[k % 2], 16)

            def load(src, c, slot, done):
                sp.dma_start(stream32[:, slot, :, :].rearrange("p t n -> p (t n)"),
                             src[bass.ds(c, 1), :, :, :].rearrange("a p t n -> p (a t n)")).then_inc(done, 16)

            for k in range(LOADS):
                sp.wait_ge(nat_saved[k], 32 * NG)
            sp.wait_ge(pv_done, NG * PAIRS)
            for slot in range(2):
                load(adj8, slot, slot, l1_loaded[slot])
            with sp.Fori(1, NG // 2) as i:
                for slot in range(2):
                    sp.wait_ge(l1_summed, 2 * i + slot - 1)
                    load(adj8, 2 * i + slot, slot, l1_loaded[slot])
            for k in range(2):
                sp.wait_ge(stage_saved[k], 16 * NG * LOADS // 2)
            for n, s in enumerate(agg):
                before = l1_summed if n == 0 else agg[0]["summed"]
                for slot in range(2):
                    sp.wait_ge(before, NG - 1 + slot)
                    load(adjT8, slot, slot, s[f"loaded{slot}"])
                with sp.Fori(1, NG // 2) as i:
                    for slot in range(2):
                        sp.wait_ge(s["summed"], 2 * i + slot - 1)
                        load(adjT8, 2 * i + slot, slot, s[f"loaded{slot}"])

            out_v = out.rearrange("(t p) d -> p t d", p=P)
            for i in range(NG):
                sp.wait_ge(out_ready, i + 1)
                sp.dma_start(out_v[:, i * GT:(i + 1) * GT, :], xn[:, i * GT:(i + 1) * GT, :]
                             ).then_inc(out_saved, 16)
            sp.wait_ge(out_saved, 16 * NG)

        @block.gpsimd
        def _(pool):
            pool.dma_start(kc[:], att_w.rearrange("h d f -> d h f")).then_inc(w_loaded, 16)
            pool.dma_start(att_b[:].rearrange("p h s f -> p (h s f)"),
                           att_v.rearrange("h a -> (h a)").partition_broadcast(P)).then_inc(w_loaded, 16)
            nc.gpsimd.memset(ident_f[:], 0.0).then_inc(ident_step, 1)
            pool.wait_ge(ident_step, 1)
            nc.gpsimd.affine_select(out=ident_f[:], in_=ident_f[:], compare_op=ALU.not_equal, fill=1.0,
                                    base=0, pattern=[[-1, P]], channel_multiplier=1).then_inc(ident_ready, 1)
            nc.gpsimd.memset(ident_big[:], 0.0).then_inc(ident_step, 1)
            nc.gpsimd.memset(minus_w[:], 0.0).then_inc(ident_step, 1)
            pool.wait_ge(ident_step, 3)
            nc.gpsimd.affine_select(out=ident_big[:], in_=ident_big[:], compare_op=ALU.not_equal, fill=BIG,
                                    base=0, pattern=[[-1, P]], channel_multiplier=1)
            nc.gpsimd.memset(minus_w[0:1, :], -MASKED)
            nc.gpsimd.memset(ones_f[:], 1.0)
            nc.gpsimd.memset(ones_m[:], 1.0).then_inc(consts_ready, 1)

            def load(g, k):
                rows = adj[g * GW:(g + 1) * GW, k * LW:(k + 1) * LW].rearrange("(t p) n -> p t n", p=P)
                pool.dma_start(nat[:, k, :, :], rows).then_inc(nat_loaded[k], 16)

            for k in range(LOADS):
                load(0, k)
            pool.wait_ge(m4_ready, 1)
            nc.gpsimd.partition_all_reduce(top4[:], m4[:], P, bass.bass_isa.ReduceOp.max).then_inc(top4_ready, 1)
            for g in range(1, NG):
                for k in range(LOADS):
                    pool.wait_ge(mask_made, (g - 1) * PAIRS + (k + 1) * PPL)
                    pool.wait_ge(nat_saved[k], 32 * g)
                    load(g, k)

        @block.tensor
        def _(pe):
            pe.wait_ge(ident_ready, 1)

            def conv(r):
                pe.wait_ge(xT_copied, r + 1)
                if r == 0:
                    pe.wait_ge(v_ready, 1)
                if r >= 2:
                    pe.wait_ge(conv_copied, r - 1)
                for j in range(GT):
                    bank, col = 2 + 2 * (r % 2) + j // 2, (j % 2) * 256
                    last = nc.tensor.matmul(ps[:, bank, col:col + 2 * F + 4],
                                            xring[:, r % 2, 0, 0, j * P:(j + 1) * P], rhs_a[:],
                                            start=True, stop=True, skip_group_check=True)
                last.then_inc(conv_made, 1)

            for r in range(NG):
                pe.wait_ge(x_loaded[r // 2], 16)
                if r >= 2:
                    pe.wait_ge(xT_copied, r - 1)
                for j in range(GT):
                    last = nc.tensor.transpose(ps[:, r % 2, j * P:(j + 1) * P], xn[:, r * GT + j, :], ident_f[:])
                last.then_inc(xT_made, 1)
                if r >= 1:
                    conv(r - 1)
            conv(NG - 1)
            pe.wait_ge(exps_ready, 1)
            nc.tensor.transpose(ps[0:HEADS * NT, 0, 0:P], ea_n[:].rearrange("p h t -> p (h t)"),
                                ident_f[:]).then_inc(eaT_made, 1)
            pe.wait_ge(consts_ready, 1)
            pe.wait_ge(eaT_copied, 1)
            pe.wait_ge(conv_copied, NG)

            def mask(g, q):
                k, slot = q // PPL, q % 2
                if q % PPL == 0:
                    pe.wait_ge(nat_loaded[k], (g + 1) * 16)
                if not (isinstance(g, int) and g == 0 and q < 2):
                    pe.wait_ge(t_made, g * PAIRS + q - 1)
                for j in range(2):
                    bank = 2 * slot + j
                    nc.tensor.matmul(ps[:, bank, :], minus_w[:], ones_m[:], start=True, stop=False)
                    col = (2 * (q % PPL) + j) * P
                    for i in range(GT):
                        last = nc.tensor.matmul(ps[:, bank, i * P:(i + 1) * P], nat[:, k, i, col:col + P],
                                                ident_big[:], start=False, stop=i == GT - 1)
                last.then_inc(mask_made, 1)

            def weigh(g, q):
                pe.wait_ge(p_made, g * PAIRS + q + 1)
                if q == 0 and not (isinstance(g, int) and g == 0):
                    pe.wait_ge(acc_copied, g)
                for h in range(HEADS):
                    for j in range(2):
                        last = nc.tensor.matmul(ps[0:FX, 4 + h, :], convx[:, 2 * q + j, h, :],
                                                xring[:, q % XB, j, h, :],
                                                start=(q == 0 and j == 0), stop=(q == PAIRS - 1 and j == 1))
                last.then_inc(pv_done, 1)

            def back(g):
                pe.wait_ge(acc_copied, g + 1)
                if not (isinstance(g, int) and g == 0):
                    pe.wait_ge(att_chain, g * (4 + LN_LINKS))
                for h in range(HEADS):
                    for i in range(GT):
                        last = nc.tensor.transpose(ps[:, 6 + h, i * P:i * P + FX], oT[:, h, i * P:(i + 1) * P],
                                                   ident_f[0:FX, 0:FX])
                last.then_inc(back_made, 1)

            def group(g, first, final):
                for q in range(PAIRS):
                    if q + 2 < PAIRS:
                        mask(g, q + 2)
                    elif not final:
                        mask(g + 1, q + 2 - PAIRS)
                    weigh(g, q)
                    if q == 1 and not first:
                        back(g - 1)

            mask(0, 0)
            mask(0, 1)
            group(0, True, False)
            with pe.Fori(1, NG - 1) as g:
                group(g, False, False)
            group(NG - 1, False, True)
            back(NG - 1)

            def hyper(i, slot):
                pe.wait_ge(l1_loaded[slot], (i + 1) * 16)
                if not (isinstance(i, int) and i == 0):
                    pe.wait_ge(l1_taken, 2 * i + slot - 1)
                pe.sem_inc(passed, 1)
                for e in range(GT):
                    for t in range(NT):
                        last = nc.tensor.matmul(ps[:, 4 * slot + e, 0:2 * D + 1],
                                                stream[:, slot, t, e * P:(e + 1) * P], parts_a[:, t, :],
                                                start=t == 0, stop=t == NT - 1)
                last.then_inc(l1_summed, 1)

            pe.wait_ge(parts1_ready, NG)
            hyper(0, 0)
            hyper(0, 1)
            with pe.Fori(1, NG // 2) as i:
                hyper(i, 0)
                hyper(i, 1)

            def neighbours(s, parts, i, slot):
                pe.wait_ge(s[f"loaded{slot}"], (i + 1) * 16)
                if not (isinstance(i, int) and i == 0):
                    pe.wait_ge(s["sT_copied"], 2 * i + slot - 1)
                pe.sem_inc(passed, 1)
                for t in range(NT):
                    for half in range(2):
                        last = nc.tensor.matmul(ps[:, slot, :], parts[:, t, half * D:(half + 1) * D],
                                                stream[:, slot, t, :], start=t == 0 and half == 0,
                                                stop=t == NT - 1 and half == 1)
                last.then_inc(s["summed"], 1)

            def xpose(s, c, slot):
                pe.wait_ge(s["staged"], c + 1)
                if not (isinstance(c, int) and c < 2):
                    pe.wait_ge(s["xT_copied"], c - 1)
                for j in range(GT):
                    last = nc.tensor.transpose(ps[:, 2 + slot, j * P:(j + 1) * P], xs[:, slot, j * P:(j + 1) * P],
                                               ident_f[:])
                last.then_inc(s["xT_made"], 1)

            def column_sums(s, c):
                pe.wait_ge(s["taken"], c + 1)
                for j in range(GT):
                    last = nc.tensor.matmul(ps[:, 6, 0:D], ones_f[:],
                                            act3[:, bass.ds(c * GT + j, 1), :].rearrange("p a d -> p (a d)"),
                                            start=isinstance(c, int) and c == 0 and j == 0,
                                            stop=isinstance(c, int) and c == NG - 1 and j == GT - 1)
                last.then_inc(s["colsum"], 1)

            def product(s, w, c, slot):
                pe.wait_ge(s["xT_copied"], c + 1)
                pe.wait_ge(s["sT_copied"], c + 1)
                if not (isinstance(c, int) and c < 2):
                    pe.wait_ge(s["taken"], c - 1)
                for j in range(GT):
                    cols = slice(j * P, (j + 1) * P)
                    nc.tensor.matmul(ps[:, 4 + slot, cols], xT[:, slot, cols], w[:, 0, :], start=True, stop=False)
                    last = nc.tensor.matmul(ps[:, 4 + slot, cols], sT[:, slot, cols], w[:, 1, :],
                                            start=False, stop=True)
                last.then_inc(s["product"], 1)

            for n, s in enumerate(agg):
                parts, w = ((parts_b, w2s), (parts_a, w3s))[n]
                if n == 0:
                    pe.wait_ge(parts2_ready, NG)
                    pe.wait_ge(l1_taken, NG)
                    pe.wait_ge(w23_loaded, 48)
                else:
                    pe.wait_ge(agg[0]["parts_out"], NG)
                    pe.wait_ge(w3_ready, 1)
                neighbours(s, parts, 0, 0)
                xpose(s, 0, 0)
                neighbours(s, parts, 0, 1)
                product(s, w, 0, 0)
                if n == 1:
                    column_sums(s, 0)
                with pe.Fori(1, NG // 2) as i:
                    xpose(s, 2 * i - 1, 1)
                    neighbours(s, parts, i, 0)
                    product(s, w, 2 * i - 1, 1)
                    xpose(s, 2 * i, 0)
                    neighbours(s, parts, i, 1)
                    product(s, w, 2 * i, 0)
                    if n == 1:
                        column_sums(s, 2 * i - 1)
                        column_sums(s, 2 * i)
                xpose(s, NG - 1, 1)
                product(s, w, NG - 1, 1)
            column_sums(agg[1], NG - 1)

            pe.wait_ge(squares, NG)
            nc.tensor.matmul(ps[:, 7, 0:NG], ones_f[:], sq[:], start=True, stop=True).then_inc(total_made, 1)

        @block.scalar
        def _(act):
            for r in range(NG):
                act.wait_ge(xT_made, r + 1)
                if r >= 2:
                    act.wait_ge(conv_made, r - 1)
                nc.scalar.activation(xring[:, r % 2, 0, 0, :], ps[:, r % 2, :], ACT.Copy).then_inc(xT_copied, 1)
            act.wait_ge(guard_ready, 1)
            for h in range(HEADS):
                last = nc.scalar.activation(ea_n[:, h, :], ab[:, :, 2 * h], ACT.Exp, bias=guard[:, h:h + 1])
            last.then_inc(exps_ready, 1)
            for h in range(HEADS):
                nc.scalar.activation(eb[:, :, h], ab[:, :, 2 * h + 1], ACT.Exp, bias=guard[:, 2 + h:3 + h])
            nc.scalar.activation(guard[:, 7:8], guard[:, 4:5], ACT.Exp)
            nc.scalar.activation(guard[:, 8:9], guard[:, 9:10], ACT.Exp).then_inc(eb_ready, 1)
            act.wait_ge(eaT_made, 1)
            nc.scalar.activation(eaT[:], ps[0:HEADS * NT, 0, 0:P], ACT.Copy).then_inc(eaT_copied, 1)
            act.wait_ge(eb_ready, 1)

            def keep(g, q):
                k, slot = q // PPL, q % 2
                act.wait_ge(mask_made, g * PAIRS + q + 1)
                if q % PPL == 0 and not (isinstance(g, int) and g == 0 and k < 2):
                    act.wait_ge(stage_saved[k % 2], g * 32 + 16 * (k // 2))
                act.sem_inc(passed, 1)
                nc.scalar.activation(stage8[:, k % 2, 2 * (q % PPL):2 * (q % PPL) + 2, :],
                                     ps[:, 2 * slot:2 * slot + 2, :], ACT.Relu, scale=1.0 / BIG,
                                     saturate=False).then_inc(mask_kept, 1)

            def expo(g, q):
                act.wait_ge(t_made, g * PAIRS + q + 1)
                n = g * PAIRS + q
                if not (isinstance(g, int) and n < EB):
                    act.wait_ge(p_made, n + 1 - EB)
                nc.scalar.activation(ering[:, q % EB, :, :, :].rearrange("p j h n -> p (j h n)"),
                                     xring[:, q % XB, :, :, :].rearrange("p j h n -> p (j h n)"),
                                     ACT.Exp, bias=guard[:, 5:6], scale=guard[:, 8:9]).then_inc(e_made, 1)

            def sums(g):
                act.wait_ge(pv_done, (g + 1) * PAIRS)
                if not (isinstance(g, int) and g == 0):
                    act.wait_ge(back_made, g)
                nc.scalar.activation(oT[:], ps[0:FX, 4:6, :], ACT.Copy).then_inc(acc_copied, 1)

            def group(g, first, final):
                for q in range(PAIRS):
                    if q + 1 < PAIRS:
                        keep(g, q + 1)
                    elif not final:
                        keep(g + 1, 0)
                    expo(g, q)
                    if q == 1 and not first:
                        sums(g - 1)

            keep(0, 0)
            group(0, True, False)
            with act.Fori(1, NG - 1) as g:
                group(g, False, False)
            group(NG - 1, False, True)
            sums(NG - 1)

            def low(c, slot):
                act.wait_ge(l1_summed, c + 1)
                if not (isinstance(c, int) and c < 2):
                    act.wait_ge(l1_taken, c - 1)
                nc.scalar.activation(tmp[:, slot, :, :], ps[:, 4 * slot:4 * slot + 4, D:2 * D],
                                     ACT.Copy).then_inc(l1_low, 1)

            low(0, 0)
            low(1, 1)
            with act.Fori(1, NG // 2) as i:
                low(2 * i, 0)
                low(2 * i + 1, 1)

            def chunk(s, c, slot):
                early = isinstance(c, int) and c < 2
                if not early:
                    act.wait_ge(s["xT_made"], c - 1)
                nc.scalar.activation(xs[:, slot, :], xn[:, bass.ds(c * GT, GT), :].rearrange("p t d -> p (t d)"),
                                     ACT.Copy).then_inc(s["staged"], 1)
                act.wait_ge(s["summed"], c + 1)
                if not early:
                    act.wait_ge(s["product"], c - 1)
                nc.scalar.activation(sT[:, slot, :], ps[:, slot, :], ACT.Copy, scale=1.0 / HL
                                     ).then_inc(s["sT_copied"], 1)
                act.wait_ge(s["xT_made"], c + 1)
                nc.scalar.activation(xT[:, slot, :], ps[:, 2 + slot, :], ACT.Copy).then_inc(s["xT_copied"], 1)

            for n, s in enumerate(agg):
                act.wait_ge(parts2_ready if n == 0 else agg[0]["parts_out"], NG)
                if n == 1:
                    act.wait_ge(agg[0]["product"], NG)
                chunk(s, 0, 0)
                chunk(s, 1, 1)
                with act.Fori(1, NG // 2) as i:
                    chunk(s, 2 * i, 0)
                    chunk(s, 2 * i + 1, 1)

            for i in range(NG):
                act.wait_ge(mean_copied, i + 1)
                nc.scalar.activation(sq_junk[:, i, :], act3[:, i * GT:(i + 1) * GT, :].rearrange("p t d -> p (t d)"),
                                     ACT.Square,
                                     accum_out=sq[:, i:i + 1]).then_inc(squares, 1)

        @block.vector
        def _(dve):
            def linker(chain, base):
                k = [0]

                def link(ins):
                    k[0] += 1
                    ins.then_inc(chain, 1)
                    dve.wait_ge(chain, base + k[0])
                return link

            link = linker(pro_chain, 0)
            nc.vector.memset(convx[:, :, :, F:FX], 1.0)
            nc.vector.memset(parts_a[:, :, 2 * D:2 * D + 1], 1.0)
            dve.wait_ge(w_loaded, 32)
            for s_ in range(2):
                last = nc.vector.tensor_tensor(vprod[:, :, s_, :], kc[:], att_b[:, :, s_, :], ALU.mult)
            link(last)
            nc.vector.tensor_copy(rhs_a[:, 0:2 * F], kc[:].rearrange("p h f -> p (h f)"))
            nc.vector.reduce_sum(rhs_a[:, 2 * F:2 * F + 4], vprod[:].rearrange("p h s f -> p (h s) f"),
                                 AX.X).then_inc(v_ready, 1)
            for r in range(NG):
                dve.wait_ge(conv_made, r + 1)
                both = ps[:, 2 + 2 * (r % 2):4 + 2 * (r % 2), :].rearrange("p b (j c) -> p (b j) c", j=2)
                for h in range(HEADS):
                    nc.vector.tensor_copy(convx[:, r * GT:(r + 1) * GT, h, 0:F], both[:, :, h * F:(h + 1) * F])
                nc.vector.tensor_copy(ab[:, r * GT:(r + 1) * GT, :], both[:, :, 2 * F:2 * F + 4]
                                      ).then_inc(conv_copied, 1)
            dve.wait_ge(conv_copied, NG)
            nc.vector.reduce_max(m4[:], ab[:].rearrange("p t k -> p k t"), AX.X).then_inc(m4_ready, 1)
            dve.wait_ge(w23_loaded, 48)
            nc.vector.tensor_tensor(w3s[:, 0, :], w3s[:, 0, :], w3s[:, 1, :], ALU.add).then_inc(w3_ready, 1)

            dve.wait_ge(top4_ready, 1)
            tops = top4[:].rearrange("p (h s) -> p h s", s=2)
            nc.vector.tensor_scalar(guard[:, 0:2], tops[:, :, 0], -1.0, None, ALU.mult)
            link(nc.vector.tensor_tensor(guard[:, 10:12], tops[:, :, 0], tops[:, :, 1], ALU.add))
            link(nc.vector.reduce_max(guard[:, 9:10], guard[:, 10:12], AX.X))
            link(nc.vector.tensor_scalar(guard[:, 6:7], guard[:, 9:10], -TOP, 0.0, ALU.add, ALU.max))
            nc.vector.tensor_scalar(guard[:, 2:4], tops[:, :, 0], guard[:, 6:7], None, ALU.subtract)
            nc.vector.tensor_scalar(guard[:, 4:5], guard[:, 6:7], -1.0, None, ALU.mult)
            nc.vector.tensor_scalar(guard[:, 9:10], guard[:, 6:7], 87.0, None, ALU.min)
            nc.vector.tensor_scalar(guard[:, 5:6], guard[:, 6:7], -1.0, -1.0, ALU.mult, ALU.add
                                    ).then_inc(guard_ready, 1)
            dve.wait_ge(eb_ready, 1)
            dve.wait_ge(ea_loaded, 16)

            def scores(g, q):
                dve.wait_ge(mask_kept, g * PAIRS + q + 1)
                if not (isinstance(g, int) and g == 0 and q < XB):
                    dve.wait_ge(pv_done, g * PAIRS + q + 1 - XB)
                for j in range(2):
                    for h in range(HEADS):
                        last = nc.vector.scalar_tensor_tensor(
                            out=xring[:, q % XB, j, h, :], in0=ea_row[:, h, bass.ds(g * GW, GW)],
                            scalar=eb[:, 2 * q + j, h:h + 1], in1=ps[:, 2 * (q % 2) + j, :],
                            op0=ALU.mult, op1=ALU.min)
                last.then_inc(t_made, 1)

            def weights(g, q):
                dve.wait_ge(e_made, g * PAIRS + q + 1)
                xq = xring[:, q % XB, :, :, :].rearrange("p j h n -> p (j h n)")
                nc.vector.scalar_tensor_tensor(
                    out=xq, in0=xq, scalar=guard[:, 7:8],
                    in1=ering[:, q % EB, :, :, :].rearrange("p j h n -> p (j h n)"),
                    op0=ALU.max, op1=ALU.min).then_inc(p_made, 1)

            def rsqrt(link, y, n):
                v, w = var[:, 0:n], var[:, GT:GT + n]
                bits = y.bitcast(int32)
                link(nc.vector.tensor_scalar(bits, v.bitcast(int32), 1, None, ALU.arith_shift_right))
                link(nc.vector.tensor_scalar(bits, bits, -1.0, float(0x5F3759DF), ALU.mult, ALU.add))
                for _ in range(NEWTON):
                    link(nc.vector.tensor_tensor(w, y, y, ALU.mult))
                    link(nc.vector.scalar_tensor_tensor(out=w, in0=w, scalar=-0.5, in1=v,
                                                        op0=ALU.mult, op1=ALU.mult))
                    link(nc.vector.scalar_tensor_tensor(out=y, in0=w, scalar=1.5, in1=y,
                                                        op0=ALU.add, op1=ALU.mult))

            def layer_norm(link, t0):
                tiles = xn[:, bass.ds(t0, GT), :]
                dve.sem_inc(passed, 1)
                for i in range(GT):
                    last = nc.vector.bn_stats(st[:, i, :], tiles[:, i, :])
                link(last)
                dve.sem_inc(passed, 1)
                for i in range(GT):
                    last = nc.vector.bn_aggr(mv[:, i, :], st[:, i, :])
                link(last)
                link(nc.vector.tensor_scalar(var[:, 0:GT], mv[:, :, 1], EPS, None, ALU.add))
                rsqrt(link, rstd[:], GT)
                for i in range(GT):
                    last = nc.vector.tensor_scalar(tiles[:, i, :], tiles[:, i, :], mv[:, i, 0:1], rstd[:, i:i + 1],
                                                   ALU.subtract, ALU.mult)
                return last

            def split(link, parts, t0, ready):
                tiles = xn[:, bass.ds(t0, GT), :]
                high = parts[:, bass.ds(t0, GT), 0:D]
                link(nc.vector.tensor_scalar(high, tiles, HL, None, ALU.mult))
                nc.vector.scalar_tensor_tensor(out=parts[:, bass.ds(t0, GT), D:2 * D], in0=tiles, scalar=HL,
                                               in1=high, op0=ALU.mult, op1=ALU.subtract).then_inc(ready, 1)

            def finish(g):
                link = linker(att_chain, g * (4 + LN_LINKS))
                dve.wait_ge(back_made, g + 1)
                sums = ps[:, 6:8, :].rearrange("p h (i c) -> p h i c", c=P)
                link(nc.vector.reciprocal(rden[:], sums[:, :, :, F]))
                for i in range(GT):
                    for h in range(HEADS):
                        node = xn[:, bass.ds(g * GT + i, 1), h * F:(h + 1) * F].rearrange("p a d -> p (a d)")
                        last = nc.vector.scalar_tensor_tensor(out=node, in0=sums[:, h, i, 0:F],
                                                              scalar=rden[:, h, i:i + 1], in1=node,
                                                              op0=ALU.mult, op1=ALU.add)
                link(last)
                link(layer_norm(link, g * GT))
                split(link, parts_a, g * GT, parts1_ready)

            def group(g, first, final):
                for q in range(PAIRS):
                    if q + 1 < PAIRS:
                        scores(g, q + 1)
                    elif not final:
                        scores(g + 1, 0)
                    weights(g, q)
                    if q == 3 and not first:
                        finish(g - 1)

            scores(0, 0)
            group(0, True, False)
            with dve.Fori(1, NG - 1) as g:
                group(g, False, False)
            group(NG - 1, False, True)
            finish(NG - 1)

            def hyper(c, slot):
                link = linker(l1_chain, c * (7 + LN_LINKS))
                dve.wait_ge(l1_summed, c + 1)
                dve.wait_ge(l1_low, c + 1)
                banks = ps[:, 4 * slot:4 * slot + 4, :]
                nc.vector.tensor_tensor(msg[:, slot, :, :], tmp[:, slot, :, :], banks[:, :, 0:D], ALU.add)
                link(nc.vector.tensor_scalar(deg[:, 0, :], banks[:, :, 2 * D], 0.0, None, ALU.is_equal))
                nc.vector.tensor_tensor(deg[:, 1, :], deg[:, 0, :], banks[:, :, 2 * D], ALU.add).then_inc(l1_taken, 1)
                dve.wait_ge(l1_taken, c + 1)
                link(nc.vector.tensor_scalar(deg[:, 2, :], deg[:, 0, :], -1.0 / HL, 1.0 / HL, ALU.mult, ALU.add))
                link(nc.vector.reciprocal(deg[:, 3, :], deg[:, 1, :]))
                link(nc.vector.tensor_tensor(deg[:, 3, :], deg[:, 3, :], deg[:, 2, :], ALU.mult))
                for i in range(GT):
                    node = xn[:, bass.ds(c * GT + i, 1), :].rearrange("p a d -> p (a d)")
                    last = nc.vector.scalar_tensor_tensor(out=node, in0=msg[:, slot, i, :],
                                                          scalar=deg[:, 3, i:i + 1], in1=node,
                                                          op0=ALU.mult, op1=ALU.add)
                link(last)
                link(layer_norm(link, c * GT))
                split(link, parts_b, c * GT, parts2_ready)

            hyper(0, 0)
            hyper(1, 1)
            with dve.Fori(1, NG // 2) as i:
                hyper(2 * i, 0)
                hyper(2 * i + 1, 1)

            def aggregate(s, c, slot):
                link = linker(s["chain"], c * (2 + LN_LINKS))
                dve.wait_ge(s["product"], c + 1)
                if s is agg[1]:
                    nc.vector.tensor_scalar(act3[:, bass.ds(c * GT, GT), :].rearrange("p t d -> p (t d)"),
                                            ps[:, 4 + slot, :], 0.0, None, ALU.max).then_inc(s["taken"], 1)
                    return
                tiles = xn[:, bass.ds(c * GT, GT), :].rearrange("p t d -> p (t d)")
                nc.vector.tensor_tensor(tiles, tiles, ps[:, 4 + slot, :], ALU.add).then_inc(s["taken"], 1)
                dve.wait_ge(s["taken"], c + 1)
                link(layer_norm(link, c * GT))
                split(link, parts_a, c * GT, s["parts_out"])

            for s in agg:
                aggregate(s, 0, 0)
                aggregate(s, 1, 1)
                with dve.Fori(1, NG // 2) as i:
                    aggregate(s, 2 * i, 0)
                    aggregate(s, 2 * i + 1, 1)

            link = linker(end_chain, 0)
            dve.wait_ge(agg[1]["colsum"], NG)
            link(nc.vector.tensor_scalar(mean_c[:], ps[:, 6, 0:D], 1.0 / N, None, ALU.mult))
            for i in range(NG):
                tiles = act3[:, i * GT:(i + 1) * GT, :]
                nc.vector.tensor_tensor(tiles, tiles, mean_c[:].unsqueeze(1).broadcast_to([P, GT, D]),
                                        ALU.subtract).then_inc(mean_copied, 1)
            dve.wait_ge(total_made, 1)
            link(nc.vector.reduce_sum(pn[:, 0:1], ps[:, 7, 0:NG], AX.X))
            link(nc.vector.tensor_scalar(var[:, 0:1], pn[:, 0:1], 1.0 / N, PAIR_EPS, ALU.mult, ALU.add))
            rsqrt(link, pn[:, 2:3], 1)
            for i in range(NG):
                tiles = xn[:, i * GT:(i + 1) * GT, :]
                link(nc.vector.scalar_tensor_tensor(out=tiles, in0=act3[:, i * GT:(i + 1) * GT, :],
                                                    scalar=pn[:, 2:3], in1=tiles, op0=ALU.mult, op1=ALU.add))
                layer_norm(link, i * GT).then_inc(out_ready, 1)


_INS = ['x', 'adj', 'L0_gnn_kernels', 'L0_gnn_att_kernels', 'L2_gnn_weight', 'L3_gnn_weight', 'L3_gnn_self_weight']


def kernel(**inputs):
    import numpy as _np
    import concourse.bacc as _bacc
    from concourse import mybir as _mybir
    from concourse.bass_utils import run_bass_kernel_spmd as _run

    nc = _bacc.Bacc("TRN2", target_bir_lowering=False, num_devices=1)
    arrays, args = {}, []
    for name in _INS:
        a = _np.ascontiguousarray(inputs[name])
        arrays[f"in_{name}"] = a
        args.append(nc.dram_tensor(f"in_{name}", a.shape, _mybir.dt.from_np(a.dtype), kind="ExternalInput").ap())
    args.append(nc.dram_tensor("out_0", inputs["x"].shape, _mybir.dt.float32, kind="ExternalOutput").ap())
    build(nc, *args)
    r = _run(nc, [arrays], core_ids=[0])
    return r.results[0]["out_0"]
```

```python
from contextlib import ExitStack

import concourse.bass as bass
from concourse import mybir


def build(nc, x, adj, att_w, att_v, w2, w3, w3_self, out):
    fp32, fp16, bf16, fp8 = mybir.dt.float32, mybir.dt.float16, mybir.dt.bfloat16, mybir.dt.float8e4
    int32 = mybir.dt.int32
    ALU, ACT, AX = mybir.AluOpType, mybir.ActivationFunctionType, mybir.AxisListType

    P = 128
    N, D = x.shape
    HEADS, _, F = att_w.shape
    NT = N // P
    GT = 4
    GW = GT * P
    NG = NT // GT
    PAIRS = NT // 2
    LOADS = 4
    LW = N // LOADS
    PPL = PAIRS // LOADS
    XB, EB, MB = 4, 2, 2
    FX = F + 1
    SPLIT, SPLIT_AT = 4, 2
    AHEAD = 3
    BIG = float(2 ** 100)
    MASKED = 127.0
    TOP = 60.0
    HL = 1024.0
    EPS = 1e-5
    NEWTON = 3
    NORM = 6 + 3 * NEWTON
    NORMALISE_AT = 13
    VECTOR_CHUNKS = (5, 7)
    ATT, HYPER = 2 + NORM, 5 + NORM
    PAIR_EPS = 1e-6

    adj8 = nc.dram_tensor("adj8", [NG, P, NT, GW // 4], fp32, kind="Internal").ap()
    adjT8 = nc.dram_tensor("adjT8", [NG, P, NT, GW // 4], fp32, kind="Internal").ap()

    ctx = ExitStack()
    with ctx:
        def sb(name, shape, dt=fp32):
            return ctx.enter_context(nc.sbuf_tensor(name, shape, dt))

        def sem(name):
            return ctx.enter_context(nc.semaphore(name))

        xn = sb("xn", [P, NT, D])
        parts_a = sb("parts_a", [P, NT, 2 * D + 1], fp16)
        convx = sb("convx", [P, NT, HEADS, FX])
        ea_row = sb("ea_row", [P, HEADS, N])
        nat = sb("nat", [P, LOADS, GT, LW], fp8)
        stage8 = sb("stage8", [P, 2, 2 * PPL, GW], fp8)
        xring = sb("xring", [P, XB, 2, HEADS, GW])
        ering = sb("ering", [P, EB, 2, HEADS, GW])
        term = sb("term", [P, HEADS, GW])
        oT = sb("oT", [FX, HEADS, GW])
        mring = sb("mring", [P, MB, 2, GW], bf16)
        stream = sb("stream", [P, 2, NT, GW], fp8)
        stream32 = stream[:].rearrange("p s t n -> p (s t n)").bitcast(fp32).rearrange(
            "p (s t n) -> p s t n", s=2, t=NT)
        xT_all = stream[:].rearrange("p s t n -> p (s t n)").bitcast(fp32)[:, 0:N]
        parts_b = ea_row[:, 0, :].bitcast(fp16).rearrange("p (t d) -> p t d", t=NT)
        act3 = ea_row[:, 1, :].rearrange("p (t d) -> p t d", t=NT)
        sq_junk = ering[:].rearrange("p a b h n -> p (a b h) n")
        rows = xring[:].rearrange("p a b h n -> p (a b h) n")
        xs, xT, sT, tmp_rows, msg_rows = (rows[:, 2 * k:2 * k + 2, :] for k in range(5))
        tmp = tmp_rows.rearrange("p s (t d) -> p s t d", t=GT)
        msg = msg_rows.rearrange("p s (t d) -> p s t d", t=GT)
        relu_sum = rows[:, 10, :]

        kc = sb("kc", [P, HEADS, F])
        att_b = sb("att_b", [P, HEADS, 2, F])
        vprod = sb("vprod", [P, HEADS, 2, F])
        rhs_a = sb("rhs_a", [P, HEADS * F + 4])
        v_wide = sb("v_wide", [P, HEADS, P])
        ab = sb("ab", [P, NT, 4])
        m4 = sb("m4", [P, 4])
        top4 = sb("top4", [P, 4])
        guard = sb("guard", [P, 15])
        eb = sb("eb", [P, NT, HEADS])
        ident_f = sb("ident_f", [P, P])
        ident_b = sb("ident_b", [P, P], bf16)
        ones_f = sb("ones_f", [P, P])
        st = sb("st", [P, GT, 6])
        mv = sb("mv", [P, GT, 2])
        rstd = sb("rstd", [P, GT])
        shift_n = sb("shift_n", [P, GT])
        var = sb("var", [P, 2, GT])
        st_all = sb("st_all", [P, NT, 6])
        mv_all = sb("mv_all", [P, NT, 2])
        var_all = sb("var_all", [P, 2, NT])
        rstd_all = sb("rstd_all", [P, NT])
        shift_all = sb("shift_all", [P, NT])
        rden = sb("rden", [P, HEADS, GT])
        deg = sb("deg", [P, 4, GT])
        w2s = sb("w2s", [P, 2, D])
        w3s = sb("w3s", [P, 2, D])
        mean_c = sb("mean_c", [P, D])
        sq = sb("sq", [P, NG])
        pn = sb("pn", [P, 4])

        ps = ctx.enter_context(nc.psum_tensor("ps", [P, 8, GW], fp32))

        passed = sem("passed")
        x_loaded = [sem(f"x_loaded{i}") for i in range(4)]
        w_loaded = sem("w_loaded")
        w23_loaded = sem("w23_loaded")
        ident_step = sem("ident_step")
        ident_ready = sem("ident_ready")
        consts_ready = sem("consts_ready")
        v_ready = sem("v_ready")
        pro_chain = sem("pro_chain")
        xT_made = sem("xT_made")
        xT_copied = sem("xT_copied")
        ab_copied = sem("ab_copied")
        conv_made = sem("conv_made")
        conv_copied = sem("conv_copied")
        m4_ready = sem("m4_ready")
        top4_ready = sem("top4_ready")
        guard_ready = sem("guard_ready")
        eb_ready = sem("eb_ready")
        split_consts = sem("split_consts")
        nat_loaded = [sem(f"nat_loaded{i}") for i in range(LOADS)]
        nat_saved = [sem(f"nat_saved{i}") for i in range(LOADS)]
        mask_made = sem("mask_made")
        mask_out = sem("mask_out")
        mask_kept = sem("mask_kept")
        ea_summed = sem("ea_summed")
        ea_made = sem("ea_made")
        stage_saved = [sem(f"stage_saved{i}") for i in range(2)]
        t_made = sem("t_made")
        e_made = sem("e_made")
        p_made = sem("p_made")
        split_step = sem("split_step")
        split_made = sem("split_made")
        pv_done = sem("pv_done")
        acc_copied = sem("acc_copied")
        back_made = sem("back_made")
        att_chain = sem("att_chain")
        att_normed = sem("att_normed")
        att_high = sem("att_high")
        parts1_ready = sem("parts1_ready")
        l1_loaded = [sem(f"l1_loaded{i}") for i in range(2)]
        l1_summed = sem("l1_summed")
        l1_low = sem("l1_low")
        l1_taken = sem("l1_taken")
        l1_chain = sem("l1_chain")
        l1_normed = sem("l1_normed")
        l1_high = sem("l1_high")
        parts2_ready = sem("parts2_ready")
        names = ("loaded0", "loaded1", "summed", "staged", "xT_made", "xT_copied", "sT_copied",
                 "product", "taken", "chain", "normed", "high", "parts_out")
        agg = [{k: sem(f"l{n}_{k}") for k in names} for n in (2, 3)]
        w3_ready = sem("w3_ready")
        end_chain = sem("end_chain")
        colsum = sem("colsum")
        squares = sem("squares")
        total_made = sem("total_made")
        mean_copied = sem("mean_copied")
        stats_ready = sem("stats_ready")
        out_ready = [sem(f"out_ready{i}") for i in range(2)]
        out_saved = sem("out_saved")

        def splits(g, q):
            return g * (PAIRS // SPLIT) + q // SPLIT + 1

        block = ctx.enter_context(nc.Block())

        @block.sync
        def _(sp):
            x_v = x.rearrange("(t p) d -> p t d", p=P)
            for i in range(4):
                sp.dma_start(xn[:, i * NT // 4:(i + 1) * NT // 4, :],
                             x_v[:, i * NT // 4:(i + 1) * NT // 4, :]).then_inc(x_loaded[i], 16)
            sp.dma_start(w2s[:], w2.rearrange("(a d) n -> d a n", a=2)).then_inc(w23_loaded, 16)
            sp.dma_start(w3s[:, 0, :], w3_self).then_inc(w23_loaded, 16)
            sp.dma_start(w3s[:, 1, :], w3).then_inc(w23_loaded, 16)

            with sp.Fori(0, NG) as g:
                for k in range(LOADS):
                    sp.wait_ge(nat_loaded[k], (g + 1) * 16)
                    for half in range(2):
                        c = 2 * k + half
                        sp.dma_start(adj8[c, :, bass.ds(g * GT, GT), :],
                                     nat[:, k, :, half * GW:(half + 1) * GW].bitcast(fp32)
                                     ).then_inc(nat_saved[k], 16)
                    sp.wait_ge(mask_kept, g * PAIRS + (k + 1) * PPL)
                    sp.dma_start(adjT8[bass.ds(g, 1), :, 2 * PPL * k:2 * PPL * (k + 1), :]
                                 .rearrange("a p t n -> p (a t n)"),
                                 stage8[:, k % 2, :, :].rearrange("p t n -> p (t n)").bitcast(fp32)
                                 ).then_inc(stage_saved[k % 2], 16)

            def load(src, c, slot, done):
                sp.dma_start(stream32[:, slot, :, :].rearrange("p t n -> p (t n)"),
                             src[bass.ds(c, 1), :, :, :].rearrange("a p t n -> p (a t n)")).then_inc(done, 16)

            for k in range(LOADS):
                sp.wait_ge(nat_saved[k], 32 * NG)
            sp.wait_ge(ea_made, NG)
            for slot in range(2):
                load(adj8, slot, slot, l1_loaded[slot])
            with sp.Fori(1, NG // 2) as i:
                for slot in range(2):
                    sp.wait_ge(l1_summed, 2 * i + slot - 1)
                    load(adj8, 2 * i + slot, slot, l1_loaded[slot])
            for k in range(2):
                sp.wait_ge(stage_saved[k], 16 * NG * LOADS // 2)
            for n, s in enumerate(agg):
                before = l1_summed if n == 0 else agg[0]["summed"]
                for slot in range(2):
                    sp.wait_ge(before, NG - 1 + slot)
                    load(adjT8, slot, slot, s[f"loaded{slot}"])
                with sp.Fori(1, NG // 2) as i:
                    for slot in range(2):
                        sp.wait_ge(s["summed"], 2 * i + slot - 1)
                        load(adjT8, 2 * i + slot, slot, s[f"loaded{slot}"])

            out_v = out.rearrange("(t p) d -> p t d", p=P)
            done = [0, 0]
            for i in range(NG):
                by = 0 if i in VECTOR_CHUNKS else 1
                done[by] += 1
                sp.wait_ge(out_ready[by], done[by])
                sp.dma_start(out_v[:, i * GT:(i + 1) * GT, :], xn[:, i * GT:(i + 1) * GT, :]
                             ).then_inc(out_saved, 16)
            sp.wait_ge(out_saved, 16 * NG)

        @block.gpsimd
        def _(pool):
            nc.gpsimd.memset(ident_f[:], 0.0).then_inc(ident_step, 1)
            nc.gpsimd.memset(ident_b[:], 0.0).then_inc(ident_step, 1)
            pool.wait_ge(ident_step, 2)
            nc.gpsimd.affine_select(out=ident_f[:], in_=ident_f[:], compare_op=ALU.not_equal, fill=1.0,
                                    base=0, pattern=[[-1, P]], channel_multiplier=1).then_inc(ident_ready, 1)
            nc.gpsimd.affine_select(out=ident_b[:], in_=ident_b[:], compare_op=ALU.not_equal, fill=1.0,
                                    base=0, pattern=[[-1, P]], channel_multiplier=1)
            nc.gpsimd.memset(ones_f[:], 1.0).then_inc(consts_ready, 1)

            def load(g, k):
                rows = adj[g * GW:(g + 1) * GW, k * LW:(k + 1) * LW].rearrange("(t p) n -> p t n", p=P)
                pool.dma_start(nat[:, k, :, :], rows).then_inc(nat_loaded[k], 16)

            for k in range(LOADS):
                load(0, k)
            pool.wait_ge(m4_ready, 1)
            nc.gpsimd.partition_all_reduce(top4[:], m4[:], P, bass.bass_isa.ReduceOp.max).then_inc(top4_ready, 1)
            for g in range(1, NG):
                for k in range(LOADS):
                    pool.wait_ge(mask_made, (g - 1) * PAIRS + (k + 1) * PPL)
                    pool.wait_ge(nat_saved[k], 32 * g)
                    load(g, k)

        @block.tensor
        def _(pe):
            pe.wait_ge(ident_ready, 1)

            def features(r):
                pe.wait_ge(xT_copied, r + 1)
                if r == 0:
                    pe.wait_ge(v_ready, 1)
                if r >= 2:
                    pe.wait_ge(conv_copied, r - 1)
                for j in range(GT):
                    bank, col, t = 2 + 2 * (r % 2) + j // 2, (j % 2) * 256, r * GT + j
                    last = nc.tensor.matmul(ps[:, bank, col:col + HEADS * F + 4], xT_all[:, t * P:(t + 1) * P],
                                            rhs_a[:], start=True, stop=True, skip_group_check=True)
                last.then_inc(conv_made, 1)

            for r in range(NG):
                pe.wait_ge(x_loaded[r // 2], 16)
                if r >= 2:
                    pe.wait_ge(xT_copied, r - 1)
                for j in range(GT):
                    last = nc.tensor.transpose(ps[:, r % 2, j * P:(j + 1) * P], xn[:, r * GT + j, :], ident_f[:])
                last.then_inc(xT_made, 1)
                if r >= 1:
                    features(r - 1)
            features(NG - 1)

            def self_terms(g, par):
                if not (isinstance(g, int) and g == 0):
                    pe.wait_ge(ea_made, g)
                if not (isinstance(g, int) and g <= 1):
                    pe.wait_ge(att_chain, (g - 2) * ATT + 2)
                for h in range(HEADS):
                    last = nc.tensor.matmul(ps[:, 4 + 2 * par + h, :], v_wide[:, h, :],
                                            xT_all[:, bass.ds(g * GW, GW)], start=True, stop=True)
                last.then_inc(ea_summed, 1)

            pe.wait_ge(xT_copied, NG)
            pe.wait_ge(consts_ready, 1)

            def mask(g, q):
                k, slot = q // PPL, q % 2
                if q % PPL == 0:
                    pe.wait_ge(nat_loaded[k], (g + 1) * 16)
                if isinstance(g, int) and g == 0 and q == 1:
                    pe.wait_ge(conv_copied, NG)
                if not (isinstance(g, int) and g == 0 and q < 2):
                    pe.wait_ge(mask_kept, g * PAIRS + q - 1)
                pe.sem_inc(passed, 1)
                for j in range(2):
                    bank = 2 * slot + j
                    col = (2 * (q % PPL) + j) * P
                    for i in range(GT):
                        last = nc.tensor.matmul(ps[:, bank, i * P:(i + 1) * P], nat[:, k, i, col:col + P],
                                                ident_b[:], start=True, stop=True, skip_group_check=True)
                last.then_inc(mask_made, 1)

            def weigh(g, q, par):
                pe.wait_ge(p_made, g * PAIRS + q + 1)

                def add(h, j, weight):
                    return nc.tensor.matmul(ps[0:FX, 4 + 2 * par + h, :], convx[:, 2 * q + j, h, :], weight,
                                            start=(q == 0 and j == 0), stop=(q == PAIRS - 1 and j == 1))
                for h in range(HEADS):
                    last = add(h, 0, xring[:, q % XB, 0, h, :])
                if q % SPLIT == SPLIT_AT:
                    pe.wait_ge(split_made, splits(g, q))
                    for h in range(HEADS):
                        last = add(h, 1, term[:, h, :])
                for h in range(HEADS):
                    last = add(h, 1, xring[:, q % XB, 1, h, :])
                last.then_inc(pv_done, 1)

            def back(g, par):
                pe.wait_ge(acc_copied, g + 1)
                for h in range(HEADS):
                    for i in range(GT):
                        last = nc.tensor.transpose(ps[:, 4 + 2 * par + h, i * P:i * P + FX], oT[:, h, i * P:(i + 1) * P],
                                                   ident_f[0:FX, 0:FX])
                last.then_inc(back_made, 1)

            def group(g, par, first, final):
                for q in range(PAIRS):
                    if q + AHEAD < PAIRS:
                        mask(g, q + AHEAD)
                    elif not final:
                        mask(g + 1, q + AHEAD - PAIRS)
                    if q == 8 and not final:
                        self_terms(g + 1, 1 - par)
                    weigh(g, q, par)
                    if q == 1 and not first:
                        back(g - 1, 1 - par)

            mask(0, 0)
            mask(0, 1)
            self_terms(0, 0)
            mask(0, 2)
            group(0, 0, True, False)
            with pe.Fori(0, (NG - 2) // 2) as i:
                group(2 * i + 1, 1, False, False)
                group(2 * i + 2, 0, False, False)
            group(NG - 1, 1, False, True)
            back(NG - 1, 1)

            def hyper(i, slot):
                first = isinstance(i, int) and i == 0
                pe.wait_ge(l1_loaded[slot], (i + 1) * 16)
                if not first:
                    pe.wait_ge(l1_taken, 2 * i + slot - 1)
                elif slot == 0:
                    pe.wait_ge(mask_kept, NG * PAIRS)
                else:
                    pe.wait_ge(att_chain, (NG - 1) * ATT + 2)
                pe.sem_inc(passed, 1)
                for t in range(NT):
                    if first and slot == 0 and t % GT == 0:
                        pe.wait_ge(parts1_ready, t // GT + 1)
                    for e in range(GT):
                        last = nc.tensor.matmul(ps[:, 4 * slot + e, 0:2 * D + 1],
                                                stream[:, slot, t, e * P:(e + 1) * P], parts_a[:, t, :],
                                                start=t == 0, stop=t == NT - 1)
                last.then_inc(l1_summed, 1)

            hyper(0, 0)
            hyper(0, 1)
            with pe.Fori(1, NG // 2) as i:
                hyper(i, 0)
                hyper(i, 1)

            def neighbours(s, parts, i, slot, arriving=None, before=None):
                pe.wait_ge(s[f"loaded{slot}"], (i + 1) * 16)
                if not (isinstance(i, int) and i == 0):
                    pe.wait_ge(s["sT_copied"], 2 * i + slot - 1)
                pe.sem_inc(passed, 1)
                for t in range(NT):
                    if arriving is not None and t % GT == 0:
                        pe.wait_ge(arriving, t // GT + 1)
                    if before is not None and t == NT // 4:
                        product(s, *before)
                    for half in range(2):
                        last = nc.tensor.matmul(ps[:, slot, :], parts[:, t, half * D:(half + 1) * D],
                                                stream[:, slot, t, :], start=t == 0 and half == 0,
                                                stop=t == NT - 1 and half == 1)
                last.then_inc(s["summed"], 1)

            def xpose(s, c, slot):
                pe.wait_ge(s["staged"], c + 1)
                if not (isinstance(c, int) and c < 2):
                    pe.wait_ge(s["xT_copied"], c - 1)
                for j in range(GT):
                    last = nc.tensor.transpose(ps[:, 2 + slot, j * P:(j + 1) * P], xs[:, slot, j * P:(j + 1) * P],
                                               ident_f[:])
                last.then_inc(s["xT_made"], 1)

            def product(s, w, c, slot):
                pe.wait_ge(s["xT_copied"], c + 1)
                pe.wait_ge(s["sT_copied"], c + 1)
                if not (isinstance(c, int) and c < 2):
                    pe.wait_ge(s["taken"], c - 1)
                for j in range(GT):
                    cols = slice(j * P, (j + 1) * P)
                    nc.tensor.matmul(ps[:, 4 + slot, cols], xT[:, slot, cols], w[:, 0, :], start=True, stop=False)
                    last = nc.tensor.matmul(ps[:, 4 + slot, cols], sT[:, slot, cols], w[:, 1, :],
                                            start=False, stop=True)
                last.then_inc(s["product"], 1)

            for n, s in enumerate(agg):
                parts, w = ((parts_b, w2s), (parts_a, w3s))[n]
                if n == 0:
                    pe.wait_ge(l1_taken, NG - 1)
                else:
                    pe.wait_ge(w3_ready, 1)
                neighbours(s, parts, 0, 0, parts2_ready if n == 0 else agg[0]["parts_out"])
                if n == 0:
                    pe.wait_ge(l1_taken, NG)
                    pe.wait_ge(w23_loaded, 48)
                xpose(s, 0, 0)

                def pair(i):
                    neighbours(s, parts, i, 0, before=(w, 2 * i - 1, 1))
                    xpose(s, 2 * i, 0)
                    neighbours(s, parts, i, 1, before=(w, 2 * i, 0))
                    xpose(s, 2 * i + 1, 1)

                neighbours(s, parts, 0, 1, before=(w, 0, 0))
                xpose(s, 1, 1)
                pair(1)
                with pe.Fori(2, NG // 2) as i:
                    pair(i)
                product(s, w, NG - 1, 1)

            pe.wait_ge(agg[1]["chain"], NG)
            for j in range(GT):
                last = nc.tensor.matmul(ps[:, 6, 0:D], ones_f[:], relu_sum[:, j * D:(j + 1) * D],
                                        start=j == 0, stop=j == GT - 1)
            last.then_inc(colsum, 1)
            pe.wait_ge(squares, NG)
            nc.tensor.matmul(ps[:, 7, 0:NG], ones_f[:], sq[:], start=True, stop=True).then_inc(total_made, 1)

        @block.scalar
        def _(act):
            act.dma_start(kc[:], att_w.rearrange("h d f -> d h f")).then_inc(w_loaded, 16)
            act.dma_start(att_b[:].rearrange("p h s f -> p (h s f)"),
                          att_v.rearrange("h a -> (h a)").partition_broadcast(P)).then_inc(w_loaded, 16)
            for r in range(NG):
                act.wait_ge(xT_made, r + 1)
                nc.scalar.activation(xT_all[:, r * GW:(r + 1) * GW], ps[:, r % 2, :], ACT.Copy
                                     ).then_inc(xT_copied, 1)
            act.wait_ge(guard_ready, 1)

            def self_exps(g, par):
                act.wait_ge(ea_summed, g + 1)
                act.sem_inc(passed, 1)
                for h in range(HEADS):
                    last = nc.scalar.activation(ea_row[:, h, bass.ds(g * GW, GW)], ps[:, 4 + 2 * par + h, :], ACT.Exp,
                                                bias=guard[:, h:h + 1])
                last.then_inc(ea_made, 1)

            for h in range(HEADS):
                nc.scalar.activation(eb[:, :, h], ab[:, :, 2 * h + 1], ACT.Exp, bias=guard[:, 2 + h:3 + h])
            nc.scalar.activation(guard[:, 7:8], guard[:, 4:5], ACT.Exp)
            nc.scalar.activation(guard[:, 8:9], guard[:, 9:10], ACT.Exp).then_inc(eb_ready, 1)
            self_exps(0, 0)
            act.wait_ge(eb_ready, 1)
            nc.scalar.activation(guard[:, 12:13], guard[:, 8:9], ACT.Copy, scale=-1.0)
            nc.scalar.activation(guard[:, 14:15], guard[:, 7:8], ACT.Copy, scale=-1.0).then_inc(split_consts, 1)
            act.wait_ge(split_consts, 1)

            def keep(g, q):
                k, slot = q // PPL, q % 2
                act.wait_ge(mask_made, g * PAIRS + q + 1)
                if not (isinstance(g, int) and g == 0 and q < MB):
                    act.wait_ge(t_made, g * PAIRS + q + 1 - MB)
                nc.scalar.activation(mring[:, q % MB, :, :], ps[:, 2 * slot:2 * slot + 2, :], ACT.Copy,
                                     scale=BIG, bias=-MASKED).then_inc(mask_out, 1)
                if q % PPL == 0 and not (isinstance(g, int) and g == 0 and k < 2):
                    act.wait_ge(stage_saved[k % 2], g * 32 + 16 * (k // 2))
                    act.sem_inc(passed, 1)
                nc.scalar.activation(stage8[:, k % 2, 2 * (q % PPL):2 * (q % PPL) + 2, :],
                                     ps[:, 2 * slot:2 * slot + 2, :], ACT.Copy, saturate=False
                                     ).then_inc(mask_kept, 1)

            def expo(g, q):
                act.wait_ge(t_made, g * PAIRS + q + 1)
                n = g * PAIRS + q
                if not (isinstance(g, int) and n < EB):
                    act.wait_ge(p_made, n + 1 - EB)
                split = q % SPLIT == SPLIT_AT
                tiles = 1 if split else 2
                nc.scalar.activation(ering[:, q % EB, 0:tiles, :, :].rearrange("p j h n -> p (j h n)"),
                                     xring[:, q % XB, 0:tiles, :, :].rearrange("p j h n -> p (j h n)"),
                                     ACT.Exp, bias=guard[:, 5:6], scale=guard[:, 8:9]).then_inc(e_made, 1)
                if split:
                    if not (isinstance(g, int) and n < SPLIT):
                        act.wait_ge(pv_done, n + 1 - SPLIT)
                    t = xring[:, q % XB, 1, :, :].rearrange("p h n -> p (h n)")
                    part = term[:].rearrange("p h n -> p (h n)")
                    nc.scalar.activation(part, t, ACT.Relu, bias=guard[:, 13:14], scale=guard[:, 12:13]
                                         ).then_inc(split_step, 1)
                    nc.scalar.activation(t, t, ACT.Relu, bias=guard[:, 14:15])
                    act.wait_ge(split_step, splits(g, q))
                    nc.scalar.activation(part, part, ACT.Exp, bias=guard[:, 4:5], scale=-1.0
                                         ).then_inc(split_made, 1)

            def sums(g, par):
                act.wait_ge(pv_done, (g + 1) * PAIRS)
                if not (isinstance(g, int) and g == 0):
                    act.wait_ge(back_made, g)
                nc.scalar.activation(oT[:], ps[0:FX, 4 + 2 * par:6 + 2 * par, :], ACT.Copy).then_inc(acc_copied, 1)

            def normalise(chain, steps, normed, high, parts, c):
                act.wait_ge(chain, steps)
                act.sem_inc(passed, 1)
                for i in range(GT):
                    node = xn[:, bass.ds(c * GT + i, 1), :].rearrange("p a d -> p (a d)")
                    last = nc.scalar.activation(node, node, ACT.Identity, scale=rstd[:, i:i + 1],
                                                bias=shift_n[:, i:i + 1])
                last.then_inc(normed, 1)
                act.wait_ge(normed, c + 1)
                act.sem_inc(passed, 1)
                nc.scalar.activation(parts[:, bass.ds(c * GT, GT), 0:D], xn[:, bass.ds(c * GT, GT), :], ACT.Copy,
                                     scale=HL).then_inc(high, 1)

            def finish(g):
                normalise(att_chain, (g + 1) * ATT, att_normed, att_high, parts_a, g)

            def group(g, par, first, final):
                for q in range(PAIRS):
                    if q + 1 < PAIRS:
                        keep(g, q + 1)
                    elif not final:
                        keep(g + 1, 0)
                    expo(g, q)
                    if q == 1 and not first:
                        sums(g - 1, 1 - par)
                    if q == 10 and not final:
                        self_exps(g + 1, 1 - par)
                    if q == NORMALISE_AT and not first:
                        finish(g - 1)

            keep(0, 0)
            group(0, 0, True, False)
            with act.Fori(0, (NG - 2) // 2) as i:
                group(2 * i + 1, 1, False, False)
                group(2 * i + 2, 0, False, False)
            group(NG - 1, 1, False, True)
            sums(NG - 1, 1)
            finish(NG - 1)

            def low(c, slot):
                act.wait_ge(l1_summed, c + 1)
                if not (isinstance(c, int) and c < 2):
                    act.wait_ge(l1_taken, c - 1)
                nc.scalar.activation(tmp[:, slot, :, :], ps[:, 4 * slot:4 * slot + 4, D:2 * D],
                                     ACT.Copy).then_inc(l1_low, 1)
                normalise(l1_chain, (c + 1) * HYPER, l1_normed, l1_high, parts_b, c)

            low(0, 0)
            low(1, 1)
            with act.Fori(1, NG // 2) as i:
                low(2 * i, 0)
                low(2 * i + 1, 1)

            def norm_before(s, c):
                normalise(s["chain"], (c + 1) * NORM, s["normed"], s["high"], parts_a, c)

            def chunk(s, c, slot):
                early = isinstance(c, int) and c < 2
                if not early:
                    act.wait_ge(s["xT_made"], c - 1)
                act.sem_inc(passed, 1)
                nc.scalar.activation(xs[:, slot, :], xn[:, bass.ds(c * GT, GT), :].rearrange("p t d -> p (t d)"),
                                     ACT.Copy).then_inc(s["staged"], 1)
                act.wait_ge(s["summed"], c + 1)
                if not early:
                    act.wait_ge(s["product"], c - 1)
                nc.scalar.activation(sT[:, slot, :], ps[:, slot, :], ACT.Copy, scale=1.0 / HL
                                     ).then_inc(s["sT_copied"], 1)
                act.wait_ge(s["xT_made"], c + 1)
                nc.scalar.activation(xT[:, slot, :], ps[:, 2 + slot, :], ACT.Copy).then_inc(s["xT_copied"], 1)

            for n, s in enumerate(agg):
                act.wait_ge(l1_normed if n == 0 else agg[0]["normed"], NG)
                if n == 1:
                    act.wait_ge(agg[0]["product"], NG)
                chunk(s, 0, 0)
                chunk(s, 1, 1)
                if n == 0:
                    norm_before(s, 0)
                with act.Fori(1, NG // 2) as i:
                    chunk(s, 2 * i, 0)
                    if n == 0:
                        norm_before(s, 2 * i - 1)
                    chunk(s, 2 * i + 1, 1)
                    if n == 0:
                        norm_before(s, 2 * i)
                if n == 0:
                    norm_before(s, NG - 1)

            for i in range(NG):
                act.wait_ge(mean_copied, i + 1)
                nc.scalar.activation(sq_junk[:, i, :], act3[:, i * GT:(i + 1) * GT, :].rearrange("p t d -> p (t d)"),
                                     ACT.Square,
                                     accum_out=sq[:, i:i + 1]).then_inc(squares, 1)
            for i in range(NG):
                if i in VECTOR_CHUNKS:
                    continue
                act.wait_ge(stats_ready, 1 + 2 * i // NG)
                for t in range(i * GT, (i + 1) * GT):
                    last = nc.scalar.activation(xn[:, t, :], xn[:, t, :], ACT.Identity, scale=rstd_all[:, t:t + 1],
                                                bias=shift_all[:, t:t + 1])
                last.then_inc(out_ready[1], 1)

        @block.vector
        def _(dve):
            def linker(chain, base):
                k = [0]

                def link(ins):
                    k[0] += 1
                    ins.then_inc(chain, 1)
                    dve.wait_ge(chain, base + k[0])
                return link

            link = linker(pro_chain, 0)
            nc.vector.memset(convx[:, :, :, F:FX], 1.0)
            nc.vector.memset(parts_a[:, :, 2 * D:2 * D + 1], 1.0)
            dve.wait_ge(w_loaded, 32)
            for s_ in range(2):
                last = nc.vector.tensor_tensor(vprod[:, :, s_, :], kc[:], att_b[:, :, s_, :], ALU.mult)
            link(last)
            nc.vector.tensor_copy(rhs_a[:, 0:HEADS * F], kc[:].rearrange("p h f -> p (h f)"))
            link(nc.vector.reduce_sum(rhs_a[:, HEADS * F:HEADS * F + 4], vprod[:].rearrange("p h s f -> p (h s) f"),
                                      AX.X))
            nc.vector.tensor_copy(v_wide[:], rhs_a[:, HEADS * F:HEADS * F + 4].rearrange("p (h s) -> p h s", s=2)
                                  [:, :, 0:1].broadcast_to([P, HEADS, P])).then_inc(v_ready, 1)
            for r in range(NG):
                dve.wait_ge(conv_made, r + 1)
                both = ps[:, 2 + 2 * (r % 2):4 + 2 * (r % 2), :].rearrange("p b (j c) -> p (b j) c", j=2)
                nc.vector.tensor_copy(ab[:, r * GT:(r + 1) * GT, :], both[:, :, HEADS * F:HEADS * F + 4]
                                      ).then_inc(ab_copied, 1)
                for h in range(HEADS):
                    last = nc.vector.tensor_copy(convx[:, r * GT:(r + 1) * GT, h, 0:F], both[:, :, h * F:(h + 1) * F])
                last.then_inc(conv_copied, 1)
            dve.wait_ge(ab_copied, NG)
            nc.vector.reduce_max(m4[:], ab[:].rearrange("p t k -> p k t"), AX.X).then_inc(m4_ready, 1)

            dve.wait_ge(top4_ready, 1)
            tops = top4[:].rearrange("p (h s) -> p h s", s=2)
            nc.vector.memset(guard[:, 13:14], 1.0)
            nc.vector.tensor_scalar(guard[:, 0:2], tops[:, :, 0], -1.0, None, ALU.mult)
            link(nc.vector.tensor_tensor(guard[:, 10:12], tops[:, :, 0], tops[:, :, 1], ALU.add))
            link(nc.vector.reduce_max(guard[:, 9:10], guard[:, 10:12], AX.X))
            link(nc.vector.tensor_scalar(guard[:, 6:7], guard[:, 9:10], -TOP, 0.0, ALU.add, ALU.max))
            nc.vector.tensor_scalar(guard[:, 2:4], tops[:, :, 0], guard[:, 6:7], None, ALU.subtract)
            nc.vector.tensor_scalar(guard[:, 4:5], guard[:, 6:7], -1.0, None, ALU.mult)
            nc.vector.tensor_scalar(guard[:, 9:10], guard[:, 6:7], 87.0, None, ALU.min)
            nc.vector.tensor_scalar(guard[:, 5:6], guard[:, 6:7], -1.0, -1.0, ALU.mult, ALU.add
                                    ).then_inc(guard_ready, 1)
            dve.wait_ge(w23_loaded, 48)
            nc.vector.tensor_tensor(w3s[:, 0, :], w3s[:, 0, :], w3s[:, 1, :], ALU.add).then_inc(w3_ready, 1)

            dve.wait_ge(eb_ready, 1)

            def scores(g, q):
                dve.wait_ge(mask_out, g * PAIRS + q + 1)
                if q == 0:
                    dve.wait_ge(ea_made, g + 1)
                if not (isinstance(g, int) and g == 0 and q < XB):
                    dve.wait_ge(pv_done, g * PAIRS + q + 1 - XB)
                for j in range(2):
                    for h in range(HEADS):
                        last = nc.vector.scalar_tensor_tensor(
                            out=xring[:, q % XB, j, h, :], in0=ea_row[:, h, bass.ds(g * GW, GW)],
                            scalar=eb[:, 2 * q + j, h:h + 1], in1=mring[:, q % MB, j, :],
                            op0=ALU.mult, op1=ALU.min)
                last.then_inc(t_made, 1)

            def weights(g, q):
                dve.wait_ge(e_made, g * PAIRS + q + 1)
                tiles = 1 if q % SPLIT == SPLIT_AT else 2
                xq = xring[:, q % XB, 0:tiles, :, :].rearrange("p j h n -> p (j h n)")
                nc.vector.scalar_tensor_tensor(
                    out=xq, in0=xq, scalar=guard[:, 7:8],
                    in1=ering[:, q % EB, 0:tiles, :, :].rearrange("p j h n -> p (j h n)"),
                    op0=ALU.max, op1=ALU.min).then_inc(p_made, 1)

            def rsqrt(k, v, w, y):
                bits = y.bitcast(int32)
                if k == 0:
                    return nc.vector.tensor_scalar(bits, v.bitcast(int32), 1, None, ALU.arith_shift_right)
                if k == 1:
                    return nc.vector.tensor_scalar(bits, bits, -1.0, float(0x5F3759DF), ALU.mult, ALU.add)
                if k % 3 == 2:
                    return nc.vector.tensor_tensor(w, y, y, ALU.mult)
                if k % 3 == 0:
                    return nc.vector.scalar_tensor_tensor(out=w, in0=w, scalar=-0.5, in1=v,
                                                          op0=ALU.mult, op1=ALU.mult)
                return nc.vector.scalar_tensor_tensor(out=y, in0=w, scalar=1.5, in1=y,
                                                      op0=ALU.add, op1=ALU.mult)

            def norm_step(chain, base, t0, k):
                if k:
                    dve.wait_ge(chain, base + k)
                if k == 0:
                    dve.sem_inc(passed, 1)
                    for i in range(GT):
                        node = xn[:, bass.ds(t0 + i, 1), :].rearrange("p a d -> p (a d)")
                        last = nc.vector.bn_stats(st[:, i, :], node)
                elif k == 1:
                    dve.sem_inc(passed, 1)
                    for i in range(GT):
                        last = nc.vector.bn_aggr(mv[:, i, :], st[:, i, :])
                elif k == 2:
                    last = nc.vector.tensor_scalar(var[:, 0, :], mv[:, :, 1], EPS, None, ALU.add)
                elif k < NORM - 1:
                    last = rsqrt(k - 3, var[:, 0, :], var[:, 1, :], rstd[:])
                else:
                    last = nc.vector.scalar_tensor_tensor(out=shift_n[:], in0=mv[:, :, 0], scalar=-1.0, in1=rstd[:],
                                                          op0=ALU.mult, op1=ALU.mult)
                last.then_inc(chain, 1)

            def low_part(high, c, parts, ready):
                dve.wait_ge(high, c + 1)
                nc.vector.scalar_tensor_tensor(out=parts[:, bass.ds(c * GT, GT), D:2 * D],
                                               in0=xn[:, bass.ds(c * GT, GT), :], scalar=HL,
                                               in1=parts[:, bass.ds(c * GT, GT), 0:D],
                                               op0=ALU.mult, op1=ALU.subtract).then_inc(ready, 1)

            def finish(g, par, k):
                sums = ps[:, 4 + 2 * par:6 + 2 * par, :].rearrange("p h (i c) -> p h i c", c=P)
                if k == 0:
                    dve.wait_ge(back_made, g + 1)
                    nc.vector.reciprocal(rden[:], sums[:, :, :, F]).then_inc(att_chain, 1)
                elif k == 1:
                    dve.wait_ge(att_chain, g * ATT + 1)
                    for i in range(GT):
                        for h in range(HEADS):
                            node = xn[:, bass.ds(g * GT + i, 1), h * F:(h + 1) * F].rearrange("p a d -> p (a d)")
                            last = nc.vector.scalar_tensor_tensor(out=node, in0=sums[:, h, i, 0:F],
                                                                  scalar=rden[:, h, i:i + 1], in1=node,
                                                                  op0=ALU.mult, op1=ALU.add)
                    last.then_inc(att_chain, 1)
                elif k < ATT:
                    if k == 2:
                        dve.wait_ge(att_chain, g * ATT + 2)
                    norm_step(att_chain, g * ATT + 2, g * GT, k - 2)
                elif k == ATT:
                    low_part(att_high, g, parts_a, parts1_ready)

            def group(g, par, first, final):
                for q in range(PAIRS):
                    if q + 1 < PAIRS:
                        scores(g, q + 1)
                    elif not final:
                        scores(g + 1, 0)
                    if not first and q >= 3 and 2 * (q - 3) < ATT:
                        finish(g - 1, 1 - par, 2 * (q - 3))
                    weights(g, q)
                    if not first and q >= 3 and 2 * (q - 3) + 1 < ATT:
                        finish(g - 1, 1 - par, 2 * (q - 3) + 1)
                    if not first and q == PAIRS - 1:
                        finish(g - 1, 1 - par, ATT)

            scores(0, 0)
            group(0, 0, True, False)
            with dve.Fori(0, (NG - 2) // 2) as i:
                group(2 * i + 1, 1, False, False)
                group(2 * i + 2, 0, False, False)
            group(NG - 1, 1, False, True)
            for k in range(ATT + 1):
                finish(NG - 1, 1, k)

            def hyper(c, slot):
                link = linker(l1_chain, c * HYPER)
                dve.wait_ge(l1_summed, c + 1)
                dve.wait_ge(l1_low, c + 1)
                banks = ps[:, 4 * slot:4 * slot + 4, :]
                nc.vector.tensor_tensor(msg[:, slot, :, :], tmp[:, slot, :, :], banks[:, :, 0:D], ALU.add)
                link(nc.vector.tensor_scalar(deg[:, 0, :], banks[:, :, 2 * D], 0.0, None, ALU.is_equal))
                nc.vector.tensor_tensor(deg[:, 1, :], deg[:, 0, :], banks[:, :, 2 * D], ALU.add).then_inc(l1_taken, 1)
                dve.wait_ge(l1_taken, c + 1)
                link(nc.vector.tensor_scalar(deg[:, 2, :], deg[:, 0, :], -1.0 / HL, 1.0 / HL, ALU.mult, ALU.add))
                link(nc.vector.reciprocal(deg[:, 3, :], deg[:, 1, :]))
                link(nc.vector.tensor_tensor(deg[:, 3, :], deg[:, 3, :], deg[:, 2, :], ALU.mult))
                for i in range(GT):
                    node = xn[:, bass.ds(c * GT + i, 1), :].rearrange("p a d -> p (a d)")
                    last = nc.vector.scalar_tensor_tensor(out=node, in0=msg[:, slot, i, :],
                                                          scalar=deg[:, 3, i:i + 1], in1=node,
                                                          op0=ALU.mult, op1=ALU.add)
                link(last)
                for k in range(NORM):
                    norm_step(l1_chain, c * HYPER + 5, c * GT, k)
                low_part(l1_high, c, parts_b, parts2_ready)

            hyper(0, 0)
            hyper(1, 1)
            with dve.Fori(1, NG // 2) as i:
                hyper(2 * i, 0)
                hyper(2 * i + 1, 1)

            def aggregate(s, c, slot):
                dve.wait_ge(s["product"], c + 1)
                if s is agg[1]:
                    relu = act3[:, bass.ds(c * GT, GT), :].rearrange("p t d -> p (t d)")
                    nc.vector.tensor_scalar(relu, ps[:, 4 + slot, :], 0.0, None, ALU.max).then_inc(s["taken"], 1)
                    dve.wait_ge(s["taken"], c + 1)
                    if isinstance(c, int) and c == 0:
                        nc.vector.tensor_copy(relu_sum, relu).then_inc(s["chain"], 1)
                    else:
                        dve.wait_ge(s["chain"], c)
                        nc.vector.tensor_tensor(relu_sum, relu_sum, relu, ALU.add).then_inc(s["chain"], 1)
                    return
                tiles = xn[:, bass.ds(c * GT, GT), :].rearrange("p t d -> p (t d)")
                nc.vector.tensor_tensor(tiles, tiles, ps[:, 4 + slot, :], ALU.add).then_inc(s["taken"], 1)
                dve.wait_ge(s["taken"], c + 1)
                for k in range(NORM):
                    norm_step(s["chain"], c * NORM, c * GT, k)
                low_part(s["high"], c, parts_a, s["parts_out"])

            for s in agg:
                aggregate(s, 0, 0)
                aggregate(s, 1, 1)
                with dve.Fori(1, NG // 2) as i:
                    aggregate(s, 2 * i, 0)
                    aggregate(s, 2 * i + 1, 1)

            dve.wait_ge(colsum, 1)
            link = linker(end_chain, 0)
            link(nc.vector.tensor_scalar(mean_c[:], ps[:, 6, 0:D], 1.0 / N, None, ALU.mult))
            for i in range(NG):
                tiles = act3[:, i * GT:(i + 1) * GT, :]
                nc.vector.tensor_tensor(tiles, tiles, mean_c[:].unsqueeze(1).broadcast_to([P, GT, D]),
                                        ALU.subtract).then_inc(mean_copied, 1)
            dve.wait_ge(total_made, 1)
            link(nc.vector.reduce_sum(pn[:, 0:1], ps[:, 7, 0:NG], AX.X))
            link(nc.vector.tensor_scalar(pn[:, 1:2], pn[:, 0:1], 1.0 / N, PAIR_EPS, ALU.mult, ALU.add))
            for k in range(2 + 3 * NEWTON):
                link(rsqrt(k, pn[:, 1:2], pn[:, 2:3], pn[:, 3:4]))
            for half in range(2):
                for i in range(half * NG // 2, (half + 1) * NG // 2):
                    tiles = xn[:, i * GT:(i + 1) * GT, :]
                    link(nc.vector.scalar_tensor_tensor(out=tiles, in0=act3[:, i * GT:(i + 1) * GT, :],
                                                        scalar=pn[:, 3:4], in1=tiles, op0=ALU.mult, op1=ALU.add))
                    for t in range(i * GT, (i + 1) * GT):
                        last = nc.vector.bn_stats(st_all[:, t, :], xn[:, t, :])
                link(last)
                own = slice(half * NT // 2, (half + 1) * NT // 2)
                for t in range(own.start, own.stop):
                    last = nc.vector.bn_aggr(mv_all[:, t, :], st_all[:, t, :])
                link(last)
                link(nc.vector.tensor_scalar(var_all[:, 0, own], mv_all[:, own, 1], EPS, None, ALU.add))
                for k in range(2 + 3 * NEWTON):
                    link(rsqrt(k, var_all[:, 0, own], var_all[:, 1, own], rstd_all[:, own]))
                nc.vector.scalar_tensor_tensor(out=shift_all[:, own], in0=mv_all[:, own, 0], scalar=-1.0,
                                               in1=rstd_all[:, own], op0=ALU.mult, op1=ALU.mult
                                               ).then_inc(stats_ready, 1)
            for i in VECTOR_CHUNKS:
                for t in range(i * GT, (i + 1) * GT):
                    last = nc.vector.tensor_scalar(xn[:, t, :], xn[:, t, :], mv_all[:, t, 0:1], rstd_all[:, t:t + 1],
                                                   ALU.subtract, ALU.mult)
                last.then_inc(out_ready[0], 1)


_INS = ['x', 'adj', 'L0_gnn_kernels', 'L0_gnn_att_kernels', 'L2_gnn_weight', 'L3_gnn_weight', 'L3_gnn_self_weight']


def kernel(**inputs):
    import numpy as _np
    import concourse.bacc as _bacc
    from concourse import mybir as _mybir
    from concourse.bass_utils import run_bass_kernel_spmd as _run

    nc = _bacc.Bacc("TRN2", target_bir_lowering=False, num_devices=1)
    arrays, args = {}, []
    for name in _INS:
        a = _np.ascontiguousarray(inputs[name])
        arrays[f"in_{name}"] = a
        args.append(nc.dram_tensor(f"in_{name}", a.shape, _mybir.dt.from_np(a.dtype), kind="ExternalInput").ap())
    args.append(nc.dram_tensor("out_0", inputs["x"].shape, _mybir.dt.float32, kind="ExternalOutput").ap())
    build(nc, *args)
    r = _run(nc, [arrays], core_ids=[0])
    return r.results[0]["out_0"]
```

```python
from contextlib import ExitStack

import concourse.bass as bass
from concourse import mybir


def build(nc, x, adj, att_w, att_v, w2, w3, w3_self, out):
    fp32, fp16, bf16, fp8 = mybir.dt.float32, mybir.dt.float16, mybir.dt.bfloat16, mybir.dt.float8e4
    int32 = mybir.dt.int32
    ALU, ACT, AX = mybir.AluOpType, mybir.ActivationFunctionType, mybir.AxisListType

    P = 128
    N, D = x.shape
    HEADS, _, F = att_w.shape
    NT = N // P
    GT = 4
    GW = GT * P
    NG = NT // GT
    HALVES = 2
    BT = HALVES * GT
    BW = BT * P
    NB = NT // BT
    LOADS = NT // GT
    SLOTS = 4
    XB, EB, MB = 4, 2, 2
    FX = F + 1
    SPLIT = (6, 9, 12, 15, 23, 30)
    LAG = 2
    AHEAD = 4
    BACK_AT = 2
    BIG = float(2 ** 100)
    MASKED = 127.0
    TOP = 60.0
    HL = 1024.0
    EPS = 1e-5
    NEWTON = 3
    NORM = 6 + 3 * NEWTON
    FINISH_AT, NORMALISE_AT, LOW_AT, SELF_AT = 7, 17, 24, 26
    END_PARTS = (0, 3), (3, 6), (6, NG)
    ROOT = 4 + 3 * NEWTON
    VECTOR_CHUNKS = (6, 7)
    ATT, HYPER = 3 + NORM, 5 + NORM
    PAIR_EPS = 1e-6

    adj8 = nc.dram_tensor("adj8", [NG, P, NT, GW // 4], fp32, kind="Internal").ap()
    adjT8 = nc.dram_tensor("adjT8", [NG, P, NT, GW // 4], fp32, kind="Internal").ap()
    a_rows = nc.dram_tensor("a_rows", [4, NT, P], fp32, kind="Internal").ap()

    ctx = ExitStack()
    with ctx:
        def sb(name, shape, dt=fp32):
            return ctx.enter_context(nc.sbuf_tensor(name, shape, dt))

        def sem(name):
            return ctx.enter_context(nc.semaphore(name))

        xn = sb("xn", [P, NT, D])
        parts_a = sb("parts_a", [P, NT, 2 * D + 1], fp16)
        convx = sb("convx", [P, NT, HEADS, FX])
        ea_row = sb("ea_row", [P, HEADS, N])
        nat = sb("nat", [P, SLOTS, BT, GW], fp8)
        stage8 = sb("stage8", [P, 2, HALVES, GT, GW], fp8)
        xring = sb("xring", [P, XB, HALVES, HEADS, GW])
        ering = sb("ering", [P, EB, HALVES, HEADS, GW])
        term = sb("term", [P, HEADS, GW])
        oT = sb("oT", [FX, HALVES, HEADS, GW])
        att = sb("att", [P, HEADS, HALVES, GT, FX])
        mring = sb("mring", [P, MB, HALVES, GW], bf16)
        stream = sb("stream", [P, 2, NT, GW], fp8)
        stream32 = stream[:].rearrange("p s t n -> p (s t n)").bitcast(fp32).rearrange(
            "p (s t n) -> p s t n", s=2, t=NT)
        xT_all = stream[:].rearrange("p s t n -> p (s t n)").bitcast(fp32)[:, 0:N]
        early = stream32[:, 1, :, :].rearrange("p t n -> p (t n)")
        kc, att_b, vprod, v_wide, abT, rhs_a = (early[:, 2 * P * k:2 * P * (k + 1)] for k in range(6))
        kc = kc[:, 0:HEADS * F].rearrange("p (h f) -> p h f", h=HEADS)
        att_b = att_b.rearrange("p (h s f) -> p h s f", h=HEADS, s=2)
        vprod = vprod.rearrange("p (h s f) -> p h s f", h=HEADS, s=2)
        v_wide = v_wide.rearrange("p (h n) -> p h n", h=HEADS)
        abT, rhs_a = abT[:, 0:P], rhs_a[:, 0:HEADS * F + 4]
        parts_b = ea_row[:, 0, :].bitcast(fp16).rearrange("p (t d) -> p t d", t=NT)
        act3 = ea_row[:, 1, :].rearrange("p (t d) -> p t d", t=NT)
        sq_junk = ering[:].rearrange("p a b h n -> p (a b h) n")
        rows = xring[:].rearrange("p a b h n -> p (a b h) n")
        xs, xT, sT, tmp_rows, msg_rows = (rows[:, 2 * k:2 * k + 2, :] for k in range(5))
        tmp = tmp_rows.rearrange("p s (t d) -> p s t d", t=GT)
        msg = msg_rows.rearrange("p s (t d) -> p s t d", t=GT)
        relu_sum = rows[:, 10, :]
        w2s, w3s = (rows[:, 11, 2 * D * k:2 * D * (k + 1)].rearrange("p (a n) -> p a n", a=2) for k in range(2))
        st_all = rows[:, 12, 0:NT * 6].rearrange("p (t k) -> p t k", k=6)
        mv_all = rows[:, 13, 0:NT * 2].rearrange("p (t k) -> p t k", k=2)
        var_all = rows[:, 13, NT * 2:NT * 4].rearrange("p (k t) -> p k t", k=2)
        rstd_all, shift_all = (rows[:, 13, NT * k:NT * (k + 1)] for k in (4, 5))
        mean_c = rows[:, 14, 0:D]

        ab = sb("ab", [P, 4, NT])
        m4 = sb("m4", [P, 4])
        top4 = sb("top4", [P, 4])
        guard = sb("guard", [P, 15])
        eb = sb("eb", [P, NT, HEADS])
        ident_f = sb("ident_f", [P, P])
        ident_b = sb("ident_b", [P, P], bf16)
        ones_f = sb("ones_f", [P, P])
        st = sb("st", [P, BT, 6])
        mv = sb("mv", [P, BT, 2])
        rstd = sb("rstd", [P, BT])
        shift_n = sb("shift_n", [P, BT])
        var = sb("var", [P, 2, BT])
        rden = sb("rden", [P, HEADS * BT])
        deg = sb("deg", [P, 4, GT])
        sq = sb("sq", [P, NG])
        pn = sb("pn", [P, 4])

        ps = ctx.enter_context(nc.psum_tensor("ps", [P, 8, GW], fp32))

        passed = sem("passed")
        x_loaded = [sem(f"x_loaded{i}") for i in range(4)]
        w_loaded = sem("w_loaded")
        w23_loaded = sem("w23_loaded")
        ident_step = sem("ident_step")
        ident_ready = sem("ident_ready")
        consts_ready = sem("consts_ready")
        v_ready = sem("v_ready")
        pro_chain = sem("pro_chain")
        xT_made = sem("xT_made")
        xT_copied = sem("xT_copied")
        ab_copied = sem("ab_copied")
        abT_made = sem("abT_made")
        abT_copied = sem("abT_copied")
        a_saved = sem("a_saved")
        a_loaded = sem("a_loaded")
        conv_made = sem("conv_made")
        conv_copied = sem("conv_copied")
        m4_ready = sem("m4_ready")
        top4_ready = sem("top4_ready")
        guard_ready = sem("guard_ready")
        eb_ready = sem("eb_ready")
        scale_ready = sem("scale_ready")
        nat_loaded = [sem(f"nat_loaded{i}") for i in range(SLOTS)]
        nat_saved = [sem(f"nat_saved{i}") for i in range(SLOTS)]
        mask_made = sem("mask_made")
        mask_out = sem("mask_out")
        mask_kept = sem("mask_kept")
        ea_summed = sem("ea_summed")
        ea_made = sem("ea_made")
        stage_saved = [sem(f"stage_saved{i}") for i in range(2)]
        t_made = sem("t_made")
        e_made = sem("e_made")
        p_made = sem("p_made")
        split_step = sem("split_step")
        split_made = sem("split_made")
        pv_done = sem("pv_done")
        acc_copied = sem("acc_copied")
        back_made = sem("back_made")
        back_taken = sem("back_taken")
        att_chain = sem("att_chain")
        att_normed = sem("att_normed")
        att_high = sem("att_high")
        parts1_ready = sem("parts1_ready")
        l1_loaded = [sem(f"l1_loaded{i}") for i in range(2)]
        l1_begun = sem("l1_begun")
        l1_ahead = sem("l1_ahead")
        l1_summed = sem("l1_summed")
        l1_low = sem("l1_low")
        l1_taken = sem("l1_taken")
        l1_chain = sem("l1_chain")
        l1_normed = sem("l1_normed")
        l1_high = sem("l1_high")
        parts2_ready = sem("parts2_ready")
        names = ("loaded0", "loaded1", "summed", "staged", "xT_made", "xT_copied", "sT_copied",
                 "product", "taken", "chain", "normed", "high", "parts_out")
        agg = [{k: sem(f"l{n}_{k}") for k in names} for n in (2, 3)]
        w3_ready = sem("w3_ready")
        end_chain = sem("end_chain")
        colsum = sem("colsum")
        squares = sem("squares")
        total_made = sem("total_made")
        mean_copied = sem("mean_copied")
        stats_ready = sem("stats_ready")
        out_ready = [sem(f"out_ready{i}") for i in range(2)]
        out_saved = sem("out_saved")

        def splits(b, u):
            return b * len(SPLIT) + SPLIT.index(u) + 1

        block = ctx.enter_context(nc.Block())

        @block.sync
        def _(sp):
            x_v = x.rearrange("(t p) d -> p t d", p=P)
            for i in range(4):
                sp.dma_start(xn[:, i * NT // 4:(i + 1) * NT // 4, :],
                             x_v[:, i * NT // 4:(i + 1) * NT // 4, :]).then_inc(x_loaded[i], 16)
            sp.wait_ge(abT_copied, 1)
            sp.dma_start(a_rows.rearrange("k t p -> (k t) p"), abT).then_inc(a_saved, 16)
            sp.wait_ge(a_saved, 16)
            for h in range(HEADS):
                sp.dma_start(ea_row[:, h, BW:N], a_rows[2 * h, BT:NT, :].rearrange("t p -> (t p)")
                             .partition_broadcast(P)).then_inc(a_loaded, 16)

            def save(b, k):
                sp.wait_ge(nat_loaded[k % SLOTS], (b * (LOADS // SLOTS) + k // SLOTS + 1) * 16)
                sp.dma_start(adj8[k, :, bass.ds(b * BT, BT), :].rearrange("p t n -> p (t n)"),
                             nat[:, k % SLOTS, :, :].rearrange("p t n -> p (t n)").bitcast(fp32)
                             ).then_inc(nat_saved[k % SLOTS], 16)
                sp.wait_ge(mask_kept, b * NT + (k + 1) * GT)
                sp.dma_start(adjT8[bass.ds(b * HALVES, HALVES), :, k * GT:(k + 1) * GT, :]
                             .rearrange("a p t n -> p a (t n)"),
                             stage8[:, k % 2, :, :, :].rearrange("p a t n -> p a (t n)").bitcast(fp32)
                             ).then_inc(stage_saved[k % 2], 16)

            with sp.Fori(0, NB - 1) as b:
                for k in range(LOADS):
                    save(b, k)

            def load(src, c, slot, done):
                sp.dma_start(stream32[:, slot, :, :].rearrange("p t n -> p (t n)"),
                             src[bass.ds(c, 1), :, :, :].rearrange("a p t n -> p (a t n)")).then_inc(done, 16)

            for k in range(LOADS):
                save(NB - 1, k)
                slot = k - LOADS // 2
                if 0 <= slot < 2:
                    sp.wait_ge(nat_saved[slot], 16 * NB * LOADS // SLOTS)
                    if slot == 0:
                        sp.wait_ge(ea_made, HEADS)
                    load(adj8, slot, slot, l1_loaded[slot])
            sp.wait_ge(pv_done, NB * NT)
            sp.dma_start(w2s, w2.rearrange("(a d) n -> d a n", a=2)).then_inc(w23_loaded, 16)
            sp.dma_start(w3s[:, 0, :], w3_self).then_inc(w23_loaded, 16)
            sp.dma_start(w3s[:, 1, :], w3).then_inc(w23_loaded, 16)
            for k in range(2, SLOTS):
                sp.wait_ge(nat_saved[k], 16 * NB * LOADS // SLOTS)
            rest = NT - BT
            sp.wait_ge(l1_begun, 1)
            sp.dma_start(stream32[:, 0, 0:rest, :].rearrange("p t n -> p (t n)"),
                         adj8[2, :, 0:rest, :].rearrange("p t n -> p (t n)")).then_inc(l1_ahead, 16)
            sp.wait_ge(l1_summed, 1)
            sp.dma_start(stream32[:, 0, rest:NT, :].rearrange("p t n -> p (t n)"),
                         adj8[2, :, rest:NT, :].rearrange("p t n -> p (t n)")).then_inc(l1_loaded[0], 16)
            sp.wait_ge(l1_summed, 2)
            load(adj8, 3, 1, l1_loaded[1])
            with sp.Fori(2, NG // 2) as i:
                for slot in range(2):
                    sp.wait_ge(l1_summed, 2 * i + slot - 1)
                    load(adj8, 2 * i + slot, slot, l1_loaded[slot])
            for k in range(2):
                sp.wait_ge(stage_saved[k], 16 * NB * LOADS // 2)
            for n, s in enumerate(agg):
                before = l1_summed if n == 0 else agg[0]["summed"]
                for slot in range(2):
                    sp.wait_ge(before, NG - 1 + slot)
                    load(adjT8, slot, slot, s[f"loaded{slot}"])
                with sp.Fori(1, NG // 2) as i:
                    for slot in range(2):
                        sp.wait_ge(s["summed"], 2 * i + slot - 1)
                        load(adjT8, 2 * i + slot, slot, s[f"loaded{slot}"])

            out_v = out.rearrange("(t p) d -> p t d", p=P)
            done = [0, 0]
            for i in range(NG):
                by = 0 if i in VECTOR_CHUNKS else 1
                done[by] += 1
                sp.wait_ge(out_ready[by], done[by])
                sp.dma_start(out_v[:, i * GT:(i + 1) * GT, :], xn[:, i * GT:(i + 1) * GT, :]
                             ).then_inc(out_saved, 16)
            sp.wait_ge(out_saved, 16 * NG)

        @block.gpsimd
        def _(pool):
            nc.gpsimd.memset(ident_f[:], 0.0).then_inc(ident_step, 1)
            nc.gpsimd.memset(ident_b[:], 0.0).then_inc(ident_step, 1)
            pool.wait_ge(ident_step, 2)
            nc.gpsimd.affine_select(out=ident_f[:], in_=ident_f[:], compare_op=ALU.not_equal, fill=1.0,
                                    base=0, pattern=[[-1, P]], channel_multiplier=1).then_inc(ident_ready, 1)
            nc.gpsimd.affine_select(out=ident_b[:], in_=ident_b[:], compare_op=ALU.not_equal, fill=1.0,
                                    base=0, pattern=[[-1, P]], channel_multiplier=1)
            nc.gpsimd.memset(ones_f[:], 1.0).then_inc(consts_ready, 1)

            def load(b, k):
                rows = adj[b * BW:(b + 1) * BW, k * GW:(k + 1) * GW].rearrange("(t p) n -> p t n", p=P)
                pool.dma_start(nat[:, k % SLOTS, :, :], rows).then_inc(nat_loaded[k % SLOTS], 16)

            for k in range(SLOTS):
                load(0, k)
            pool.wait_ge(m4_ready, 1)
            nc.gpsimd.partition_all_reduce(top4[:], m4[:], P, bass.bass_isa.ReduceOp.max).then_inc(top4_ready, 1)
            for n in range(SLOTS, NB * LOADS):
                pool.wait_ge(mask_made, (n - SLOTS + 1) * GT)
                pool.wait_ge(nat_saved[n % SLOTS], 16 * (n // SLOTS))
                load(n // LOADS, n % LOADS)

        @block.tensor
        def _(pe):
            pe.wait_ge(ident_ready, 1)

            def features(r):
                pe.wait_ge(xT_copied, r + 1)
                if r == 0:
                    pe.wait_ge(v_ready, 1)
                if r >= 2:
                    pe.wait_ge(conv_copied, r - 1)
                for j in range(GT):
                    bank, col, t = 2 + 2 * (r % 2) + j // 2, (j % 2) * 256, r * GT + j
                    last = nc.tensor.matmul(ps[:, bank, col:col + HEADS * F + 4], xT_all[:, t * P:(t + 1) * P],
                                            rhs_a, start=True, stop=True, skip_group_check=True)
                last.then_inc(conv_made, 1)

            def self_terms(half):
                for h in range(HEADS):
                    last = nc.tensor.matmul(ps[:, 6 - 2 * half + h, :], v_wide[:, h, :],
                                            xT_all[:, half * GW:(half + 1) * GW], start=True, stop=True)
                last.then_inc(ea_summed, 1)

            for r in range(NG):
                if r == 3:
                    self_terms(0)
                pe.wait_ge(x_loaded[r // 2], 16)
                if r >= 2:
                    pe.wait_ge(xT_copied, r - 1)
                for j in range(GT):
                    last = nc.tensor.transpose(ps[:, r % 2, j * P:(j + 1) * P], xn[:, r * GT + j, :], ident_f[:])
                last.then_inc(xT_made, 1)
                if r >= LAG:
                    features(r - LAG)
            for r in range(NG - LAG, NG):
                features(r)

            pe.wait_ge(xT_copied, NG)
            pe.wait_ge(consts_ready, 1)

            def mask(b, u):
                k, slot = u // GT, u % 2
                late = u - BACK_AT - AHEAD
                if u % GT == 0:
                    pe.wait_ge(nat_loaded[k % SLOTS], (b * (LOADS // SLOTS) + k // SLOTS + 1) * 16)
                if isinstance(b, int) and b == 0 and u == 1:
                    pe.wait_ge(abT_copied, 1)
                if not (isinstance(b, int) and b == 0) and 0 <= late < 2:
                    pe.wait_ge(back_taken, (b - 1) * HALVES + late + 1)
                elif not (isinstance(b, int) and b == 0 and u < 2):
                    pe.wait_ge(mask_kept, b * NT + u - 1)
                pe.sem_inc(passed, 1)
                for half in range(HALVES):
                    for i in range(GT):
                        last = nc.tensor.matmul(ps[:, 2 * slot + half, i * P:(i + 1) * P],
                                                nat[:, k % SLOTS, half * GT + i, (u % GT) * P:(u % GT + 1) * P],
                                                ident_b[:], start=True, stop=True, skip_group_check=True)
                last.then_inc(mask_made, 1)

            def weigh(b, u, half):
                if half == 0:
                    pe.wait_ge(p_made, b * NT + u + 1)
                if u == 0 and not (isinstance(b, int) and b == 0):
                    pe.wait_ge(acc_copied, (b - 1) * HALVES + half + 1)

                def add(h, weight, start, stop):
                    return nc.tensor.matmul(ps[0:FX, 4 + 2 * half + h, :], convx[:, u, h, :], weight,
                                            start=start, stop=stop)
                split = half == 1 and u in SPLIT
                if split:
                    pe.wait_ge(split_made, splits(b, u))
                    for h in range(HEADS):
                        add(h, term[:, h, :], u == 0, False)
                for h in range(HEADS):
                    last = add(h, xring[:, u % XB, half, h, :], u == 0 and not split, u == NT - 1)
                if half == 1:
                    last.then_inc(pv_done, 1)

            def back(b, half, bank):
                pe.wait_ge(acc_copied, b * HALVES + half + 1)
                for h in range(HEADS):
                    for i in range(GT):
                        last = nc.tensor.transpose(ps[:, bank + h, i * P:i * P + FX], oT[:, half, h, i * P:(i + 1) * P],
                                                   ident_f[0:FX, 0:FX])
                last.then_inc(back_made, 1)

            def unit_block(b, first, final):
                for u in range(NT):
                    if not first and u == BACK_AT:
                        turns = ("back", 0), ("back", 1)
                    elif not first and u == BACK_AT + 1:
                        turns = ("mask", u + AHEAD - 1), ("mask", u + AHEAD)
                    else:
                        turns = ("mask", u + AHEAD), None
                    for half in range(HALVES):
                        if turns[half]:
                            what, n = turns[half]
                            if what == "back":
                                pe.wait_ge(mask_kept, b * NT + BACK_AT + AHEAD - 1 + half)
                                back(b - 1, n, 2 * n)
                            elif n < NT:
                                mask(b, n)
                            elif not final:
                                mask(b + 1, n - NT)
                        weigh(b, u, half)

            mask(0, 0)
            pe.wait_ge(conv_copied, NG)
            nc.tensor.transpose(ps[:, 2, 0:P], ab[:].rearrange("p k t -> p (k t)"), ident_f[:]).then_inc(abT_made, 1)
            self_terms(1)
            for u in range(1, AHEAD):
                mask(0, u)
            unit_block(0, True, False)
            with pe.Fori(1, NB - 1) as b:
                unit_block(b, False, False)
            unit_block(NB - 1, False, True)

            def members(slot, t0, t1):
                for t in range(t0, t1):
                    for e in range(GT):
                        last = nc.tensor.matmul(ps[:, 4 * slot + e, 0:2 * D + 1],
                                                stream[:, slot, t, e * P:(e + 1) * P], parts_a[:, t, :],
                                                start=t == 0, stop=t == NT - 1, skip_group_check=True)
                return last

            def hyper(i, slot):
                first = 0
                if isinstance(i, int) and i == 1 and slot == 0:
                    first = NT - BT
                    pe.wait_ge(l1_ahead, 16)
                    pe.wait_ge(l1_taken, 1)
                    pe.sem_inc(passed, 1)
                    members(slot, 0, first)
                pe.wait_ge(l1_loaded[slot], (i + 1) * 16)
                pe.wait_ge(l1_taken, 2 * i + slot - 1)
                pe.sem_inc(passed, 1)
                members(slot, first, NT).then_inc(l1_summed, 1)

            pe.wait_ge(l1_loaded[0], 16)
            pe.wait_ge(mask_kept, NB * NT)
            pe.wait_ge(parts1_ready, NB - 1)
            pe.sem_inc(passed, 1)
            members(0, 0, BT)
            for half in range(HALVES):
                back(NB - 1, half, 4 + 2 * half)
            members(0, BT, NT - BT).then_inc(l1_begun, 1)
            pe.wait_ge(l1_loaded[1], 16)
            pe.wait_ge(back_taken, NB * HALVES)
            pe.sem_inc(passed, 1)
            members(1, 0, NT - BT)
            pe.wait_ge(parts1_ready, NB)
            pe.sem_inc(passed, 1)
            members(0, NT - BT, NT).then_inc(l1_summed, 1)
            members(1, NT - BT, NT).then_inc(l1_summed, 1)
            hyper(1, 0)
            hyper(1, 1)
            with pe.Fori(2, NG // 2) as i:
                hyper(i, 0)
                hyper(i, 1)

            def neighbours(s, parts, i, slot, arriving=None, before=None):
                pe.wait_ge(s[f"loaded{slot}"], (i + 1) * 16)
                if not (isinstance(i, int) and i == 0):
                    pe.wait_ge(s["sT_copied"], 2 * i + slot - 1)
                pe.sem_inc(passed, 1)
                for t in range(NT):
                    if arriving is not None and t % GT == 0:
                        pe.wait_ge(arriving, t // GT + 1)
                    if before is not None and t == NT // 4:
                        product(s, *before)
                    for half in range(2):
                        last = nc.tensor.matmul(ps[:, slot, :], parts[:, t, half * D:(half + 1) * D],
                                                stream[:, slot, t, :], start=t == 0 and half == 0,
                                                stop=t == NT - 1 and half == 1)
                last.then_inc(s["summed"], 1)

            def xpose(s, c, slot):
                pe.wait_ge(s["staged"], c + 1)
                if not (isinstance(c, int) and c < 2):
                    pe.wait_ge(s["xT_copied"], c - 1)
                for j in range(GT):
                    last = nc.tensor.transpose(ps[:, 2 + slot, j * P:(j + 1) * P], xs[:, slot, j * P:(j + 1) * P],
                                               ident_f[:])
                last.then_inc(s["xT_made"], 1)

            def product(s, w, c, slot):
                pe.wait_ge(s["xT_copied"], c + 1)
                pe.wait_ge(s["sT_copied"], c + 1)
                if not (isinstance(c, int) and c < 2):
                    pe.wait_ge(s["taken"], c - 1)
                for j in range(GT):
                    cols = slice(j * P, (j + 1) * P)
                    nc.tensor.matmul(ps[:, 4 + slot, cols], xT[:, slot, cols], w[:, 0, :], start=True, stop=False)
                    last = nc.tensor.matmul(ps[:, 4 + slot, cols], sT[:, slot, cols], w[:, 1, :],
                                            start=False, stop=True)
                last.then_inc(s["product"], 1)

            for n, s in enumerate(agg):
                parts, w = ((parts_b, w2s), (parts_a, w3s))[n]
                if n == 0:
                    pe.wait_ge(l1_taken, NG - 1)
                else:
                    pe.wait_ge(w3_ready, 1)
                neighbours(s, parts, 0, 0, parts2_ready if n == 0 else agg[0]["parts_out"])
                if n == 0:
                    pe.wait_ge(l1_taken, NG)
                    pe.wait_ge(w23_loaded, 48)
                xpose(s, 0, 0)

                def pair(i):
                    neighbours(s, parts, i, 0, before=(w, 2 * i - 1, 1))
                    xpose(s, 2 * i, 0)
                    neighbours(s, parts, i, 1, before=(w, 2 * i, 0))
                    xpose(s, 2 * i + 1, 1)

                neighbours(s, parts, 0, 1, before=(w, 0, 0))
                xpose(s, 1, 1)
                pair(1)
                with pe.Fori(2, NG // 2) as i:
                    pair(i)
                product(s, w, NG - 1, 1)

            pe.wait_ge(agg[1]["chain"], NG)
            for j in range(GT):
                last = nc.tensor.matmul(ps[:, 6, 0:D], ones_f[:], relu_sum[:, j * D:(j + 1) * D],
                                        start=j == 0, stop=j == GT - 1)
            last.then_inc(colsum, 1)
            pe.wait_ge(squares, NG)
            nc.tensor.matmul(ps[:, 7, 0:NG], ones_f[:], sq[:], start=True, stop=True).then_inc(total_made, 1)

        @block.scalar
        def _(act):
            act.dma_start(kc, att_w.rearrange("h d f -> d h f")).then_inc(w_loaded, 16)
            act.dma_start(att_b.rearrange("p h s f -> p (h s f)"),
                          att_v.rearrange("h a -> (h a)").partition_broadcast(P)).then_inc(w_loaded, 16)
            for r in range(NG):
                act.wait_ge(xT_made, r + 1)
                nc.scalar.activation(xT_all[:, r * GW:(r + 1) * GW], ps[:, r % 2, :], ACT.Copy
                                     ).then_inc(xT_copied, 1)
            def self_exps(b, h):
                row = ea_row[:, h, bass.ds(b * BW, BW)]
                if isinstance(b, int) and b == 0:
                    act.wait_ge(ea_summed, HALVES)
                    for half in range(HALVES):
                        last = nc.scalar.activation(row[:, half * GW:(half + 1) * GW], ps[:, 6 - 2 * half + h, :],
                                                    ACT.Exp, bias=guard[:, h:h + 1])
                    last.then_inc(ea_made, 1)
                    return
                act.wait_ge(a_loaded, 16 * HEADS)
                act.sem_inc(passed, 1)
                nc.scalar.activation(row, row, ACT.Exp, bias=guard[:, h:h + 1]).then_inc(ea_made, 1)

            def keep(b, u):
                k, slot = u // GT, u % 2
                act.wait_ge(mask_made, b * NT + u + 1)
                if not (isinstance(b, int) and b == 0 and u < MB):
                    act.wait_ge(t_made, b * NT + u + 1 - MB)
                nc.scalar.activation(mring[:, u % MB, :, :], ps[:, 2 * slot:2 * slot + 2, :], ACT.Copy,
                                     scale=BIG, bias=-MASKED).then_inc(mask_out, 1)
                if u % GT == 0 and not (isinstance(b, int) and b == 0 and k < 2):
                    act.wait_ge(stage_saved[k % 2], b * (LOADS // 2) * 16 + 16 * (k // 2))
                    act.sem_inc(passed, 1)
                nc.scalar.activation(stage8[:, k % 2, :, u % GT, :], ps[:, 2 * slot:2 * slot + 2, :], ACT.Copy,
                                     saturate=False).then_inc(mask_kept, 1)

            def expo(b, u):
                act.wait_ge(t_made, b * NT + u + 1)
                n = b * NT + u
                if not (isinstance(b, int) and n < EB):
                    act.wait_ge(p_made, n + 1 - EB)
                split = u in SPLIT
                halves = 1 if split else 2
                nc.scalar.activation(ering[:, u % EB, 0:halves, :, :].rearrange("p a h n -> p (a h n)"),
                                     xring[:, u % XB, 0:halves, :, :].rearrange("p a h n -> p (a h n)"),
                                     ACT.Exp, bias=guard[:, 5:6], scale=guard[:, 8:9]).then_inc(e_made, 1)
                if split:
                    nth = SPLIT.index(u)
                    before = SPLIT[nth - 1] if nth else SPLIT[-1] - NT
                    if not (isinstance(b, int) and b * NT + before < 0):
                        act.wait_ge(pv_done, b * NT + before + 1)
                    t = xring[:, u % XB, 1, :, :].rearrange("p h n -> p (h n)")
                    part = term[:].rearrange("p h n -> p (h n)")
                    nc.scalar.activation(part, t, ACT.Relu, bias=guard[:, 13:14], scale=guard[:, 12:13]
                                         ).then_inc(split_step, 1)
                    nc.scalar.activation(t, t, ACT.Relu, bias=guard[:, 14:15])
                    act.wait_ge(split_step, splits(b, u))
                    nc.scalar.activation(part, part, ACT.Exp, bias=guard[:, 4:5], scale=-1.0
                                         ).then_inc(split_made, 1)

            def sums(b):
                act.wait_ge(pv_done, (b + 1) * NT)
                for half in range(HALVES):
                    nc.scalar.activation(oT[:, half, :, :], ps[0:FX, 4 + 2 * half:6 + 2 * half, :], ACT.Copy
                                         ).then_inc(acc_copied, 1)

            def take(b, half, bank):
                act.wait_ge(back_made, b * HALVES + half + 1)
                nc.scalar.activation(att[:, :, half, :, :],
                                     ps[:, bank:bank + 2, :].rearrange("p h (i c) -> p h i c", c=P)[:, :, :, 0:FX],
                                     ACT.Copy).then_inc(back_taken, 1)

            def normalise(chain, steps, normed, nth, high, parts, t0, tiles, piece=None):
                pieces = tiles // 2
                if not piece:
                    act.wait_ge(chain, steps)
                    act.sem_inc(passed, 1)
                if piece is None or piece < pieces:
                    for i in range(tiles) if piece is None else (2 * piece, 2 * piece + 1):
                        node = xn[:, bass.ds(t0 + i, 1), :].rearrange("p a d -> p (a d)")
                        last = nc.scalar.activation(node, node, ACT.Identity, scale=rstd[:, i:i + 1],
                                                    bias=shift_n[:, i:i + 1])
                if piece is None or piece == pieces - 1:
                    last.then_inc(normed, 1)
                if piece is None or piece == pieces:
                    act.wait_ge(normed, nth)
                    act.sem_inc(passed, 1)
                    nc.scalar.activation(parts[:, bass.ds(t0, tiles), 0:D], xn[:, bass.ds(t0, tiles), :], ACT.Copy,
                                         scale=HL).then_inc(high, 1)

            def finish(b, piece=None):
                normalise(att_chain, (b + 1) * ATT, att_normed, b + 1, att_high, parts_a, b * BT, BT, piece)

            def unit_block(b, first, final):
                for u in range(NT):
                    if u + 1 < NT:
                        keep(b, u + 1)
                    elif not final:
                        keep(b + 1, 0)
                    if not first and u == BACK_AT + 3:
                        take(b - 1, 1, 2)
                    expo(b, u)
                    if not first and u == BACK_AT - 1:
                        sums(b - 1)
                    if not first and u == BACK_AT + 2:
                        take(b - 1, 0, 0)
                    if not first and 0 <= u - NORMALISE_AT <= BT // 2:
                        finish(b - 1, u - NORMALISE_AT)
                    if not final and 0 <= u - SELF_AT < HEADS:
                        self_exps(b + 1, u - SELF_AT)

            keep(0, 0)
            act.wait_ge(abT_made, 1)
            nc.scalar.activation(abT, ps[:, 2, 0:P], ACT.Copy).then_inc(abT_copied, 1)
            act.wait_ge(guard_ready, 1)
            for h in range(HEADS):
                last = nc.scalar.activation(eb[:, :, h], ab[:, 2 * h + 1, :], ACT.Exp, bias=guard[:, 2 + h:3 + h])
            last.then_inc(eb_ready, 1)
            for h in range(HEADS):
                self_exps(0, h)
            nc.scalar.activation(guard[:, 7:8], guard[:, 4:5], ACT.Exp)
            nc.scalar.activation(guard[:, 8:9], guard[:, 9:10], ACT.Exp).then_inc(scale_ready, 1)
            act.wait_ge(scale_ready, 1)
            nc.scalar.activation(guard[:, 12:13], guard[:, 8:9], ACT.Copy, scale=-1.0)
            nc.scalar.activation(guard[:, 14:15], guard[:, 7:8], ACT.Copy, scale=-1.0).then_inc(scale_ready, 1)
            act.wait_ge(scale_ready, 2)
            unit_block(0, True, False)
            with act.Fori(1, NB - 1) as b:
                unit_block(b, False, False)
            unit_block(NB - 1, False, True)
            sums(NB - 1)
            for half in range(HALVES):
                take(NB - 1, half, 4 + 2 * half)
            finish(NB - 1)

            def low(c, slot):
                act.wait_ge(l1_summed, c + 1)
                if not (isinstance(c, int) and c < 2):
                    act.wait_ge(l1_taken, c - 1)
                nc.scalar.activation(tmp[:, slot, :, :], ps[:, 4 * slot:4 * slot + 4, D:2 * D],
                                     ACT.Copy).then_inc(l1_low, 1)
                normalise(l1_chain, (c + 1) * HYPER, l1_normed, c + 1, l1_high, parts_b, c * GT, GT)

            low(0, 0)
            low(1, 1)
            with act.Fori(1, NG // 2) as i:
                low(2 * i, 0)
                low(2 * i + 1, 1)

            def norm_before(s, c):
                normalise(s["chain"], (c + 1) * NORM, s["normed"], c + 1, s["high"], parts_a, c * GT, GT)

            def chunk(s, c, slot):
                early = isinstance(c, int) and c < 2
                if not early:
                    act.wait_ge(s["xT_made"], c - 1)
                act.sem_inc(passed, 1)
                nc.scalar.activation(xs[:, slot, :], xn[:, bass.ds(c * GT, GT), :].rearrange("p t d -> p (t d)"),
                                     ACT.Copy).then_inc(s["staged"], 1)
                act.wait_ge(s["summed"], c + 1)
                if not early:
                    act.wait_ge(s["product"], c - 1)
                nc.scalar.activation(sT[:, slot, :], ps[:, slot, :], ACT.Copy, scale=1.0 / HL
                                     ).then_inc(s["sT_copied"], 1)
                act.wait_ge(s["xT_made"], c + 1)
                nc.scalar.activation(xT[:, slot, :], ps[:, 2 + slot, :], ACT.Copy).then_inc(s["xT_copied"], 1)

            for n, s in enumerate(agg):
                act.wait_ge(l1_normed if n == 0 else agg[0]["normed"], NG)
                if n == 1:
                    act.wait_ge(agg[0]["product"], NG)
                chunk(s, 0, 0)
                chunk(s, 1, 1)
                if n == 0:
                    norm_before(s, 0)
                with act.Fori(1, NG // 2) as i:
                    chunk(s, 2 * i, 0)
                    if n == 0:
                        norm_before(s, 2 * i - 1)
                    chunk(s, 2 * i + 1, 1)
                    if n == 0:
                        norm_before(s, 2 * i)
                if n == 0:
                    norm_before(s, NG - 1)

            for i in range(NG):
                act.wait_ge(mean_copied, i + 1)
                nc.scalar.activation(sq_junk[:, i, :], act3[:, i * GT:(i + 1) * GT, :].rearrange("p t d -> p (t d)"),
                                     ACT.Square,
                                     accum_out=sq[:, i:i + 1]).then_inc(squares, 1)
            for i in range(NG):
                if i in VECTOR_CHUNKS:
                    continue
                act.wait_ge(stats_ready, 1 + sum(i >= stop for _, stop in END_PARTS))
                for t in range(i * GT, (i + 1) * GT):
                    last = nc.scalar.activation(xn[:, t, :], xn[:, t, :], ACT.Identity, scale=rstd_all[:, t:t + 1],
                                                bias=shift_all[:, t:t + 1])
                last.then_inc(out_ready[1], 1)

        @block.vector
        def _(dve):
            def linker(chain, base):
                k = [0]

                def link(ins):
                    k[0] += 1
                    ins.then_inc(chain, 1)
                    dve.wait_ge(chain, base + k[0])
                return link

            link = linker(pro_chain, 0)
            nc.vector.memset(convx[:, :, :, F:FX], 1.0)
            nc.vector.memset(parts_a[:, :, 2 * D:2 * D + 1], 1.0)
            dve.wait_ge(w_loaded, 32)
            for s_ in range(2):
                last = nc.vector.tensor_tensor(vprod[:, :, s_, :], kc, att_b[:, :, s_, :], ALU.mult)
            link(last)
            nc.vector.tensor_copy(rhs_a[:, 0:HEADS * F], kc.rearrange("p h f -> p (h f)"))
            link(nc.vector.reduce_sum(rhs_a[:, HEADS * F:HEADS * F + 4], vprod.rearrange("p h s f -> p (h s) f"),
                                      AX.X))
            nc.vector.tensor_copy(v_wide, rhs_a[:, HEADS * F:HEADS * F + 4].rearrange("p (h s) -> p h s", s=2)
                                  [:, :, 0:1].broadcast_to([P, HEADS, P])).then_inc(v_ready, 1)
            for r in range(NG):
                dve.wait_ge(conv_made, r + 1)
                both = ps[:, 2 + 2 * (r % 2):4 + 2 * (r % 2), :].rearrange("p b (j c) -> p (b j) c", j=2)
                nc.vector.tensor_copy(ab[:, :, r * GT:(r + 1) * GT].rearrange("p k t -> p t k"),
                                      both[:, :, HEADS * F:HEADS * F + 4]
                                      ).then_inc(ab_copied, 1)
                for h in range(HEADS):
                    last = nc.vector.tensor_copy(convx[:, r * GT:(r + 1) * GT, h, 0:F], both[:, :, h * F:(h + 1) * F])
                last.then_inc(conv_copied, 1)
            dve.wait_ge(ab_copied, NG)
            nc.vector.reduce_max(m4[:], ab[:], AX.X).then_inc(m4_ready, 1)

            dve.wait_ge(top4_ready, 1)
            tops = top4[:].rearrange("p (h s) -> p h s", s=2)
            nc.vector.memset(guard[:, 13:14], 1.0)
            nc.vector.tensor_scalar(guard[:, 0:2], tops[:, :, 0], -1.0, None, ALU.mult)
            link(nc.vector.tensor_tensor(guard[:, 10:12], tops[:, :, 0], tops[:, :, 1], ALU.add))
            link(nc.vector.reduce_max(guard[:, 9:10], guard[:, 10:12], AX.X))
            link(nc.vector.tensor_scalar(guard[:, 6:7], guard[:, 9:10], -TOP, 0.0, ALU.add, ALU.max))
            nc.vector.tensor_scalar(guard[:, 2:4], tops[:, :, 0], guard[:, 6:7], None, ALU.subtract)
            nc.vector.tensor_scalar(guard[:, 4:5], guard[:, 6:7], -1.0, None, ALU.mult)
            nc.vector.tensor_scalar(guard[:, 9:10], guard[:, 6:7], 87.0, None, ALU.min)
            nc.vector.tensor_scalar(guard[:, 5:6], guard[:, 6:7], -1.0, -1.0, ALU.mult, ALU.add
                                    ).then_inc(guard_ready, 1)
            dve.wait_ge(eb_ready, 1)

            def scores(b, u):
                dve.wait_ge(mask_out, b * NT + u + 1)
                if not (isinstance(b, int) and b == 0 and u < XB):
                    dve.wait_ge(pv_done, b * NT + u + 1 - XB)
                for h in range(HEADS):
                    if u == 0:
                        dve.wait_ge(ea_made, b * HEADS + h + 1)
                    last = nc.vector.scalar_tensor_tensor(
                        out=xring[:, u % XB, :, h, :],
                        in0=ea_row[:, h, bass.ds(b * BW, BW)].rearrange("p (a n) -> p a n", a=HALVES),
                        scalar=eb[:, u, h:h + 1], in1=mring[:, u % MB, :, :], op0=ALU.mult, op1=ALU.min)
                last.then_inc(t_made, 1)

            def weights(b, u):
                dve.wait_ge(e_made, b * NT + u + 1)
                halves = 1 if u in SPLIT else 2
                xu = xring[:, u % XB, 0:halves, :, :].rearrange("p a h n -> p (a h n)")
                nc.vector.scalar_tensor_tensor(
                    out=xu, in0=xu, scalar=guard[:, 7:8],
                    in1=ering[:, u % EB, 0:halves, :, :].rearrange("p a h n -> p (a h n)"),
                    op0=ALU.max, op1=ALU.min).then_inc(p_made, 1)

            def rsqrt(k, v, w, y):
                bits = y.bitcast(int32)
                if k == 0:
                    return nc.vector.tensor_scalar(bits, v.bitcast(int32), 1, None, ALU.arith_shift_right)
                if k == 1:
                    return nc.vector.tensor_scalar(bits, bits, -1.0, float(0x5F3759DF), ALU.mult, ALU.add)
                if k % 3 == 2:
                    return nc.vector.tensor_tensor(w, y, y, ALU.mult)
                if k % 3 == 0:
                    return nc.vector.scalar_tensor_tensor(out=w, in0=w, scalar=-0.5, in1=v,
                                                          op0=ALU.mult, op1=ALU.mult)
                return nc.vector.scalar_tensor_tensor(out=y, in0=w, scalar=1.5, in1=y,
                                                      op0=ALU.add, op1=ALU.mult)

            def norm_step(chain, base, t0, tiles, k):
                own = slice(0, tiles)
                if k:
                    dve.wait_ge(chain, base + k)
                if k == 0:
                    dve.sem_inc(passed, 1)
                    for i in range(tiles):
                        node = xn[:, bass.ds(t0 + i, 1), :].rearrange("p a d -> p (a d)")
                        last = nc.vector.bn_stats(st[:, i, :], node)
                elif k == 1:
                    dve.sem_inc(passed, 1)
                    for i in range(tiles):
                        last = nc.vector.bn_aggr(mv[:, i, :], st[:, i, :])
                elif k == 2:
                    last = nc.vector.tensor_scalar(var[:, 0, own], mv[:, own, 1], EPS, None, ALU.add)
                elif k < NORM - 1:
                    last = rsqrt(k - 3, var[:, 0, own], var[:, 1, own], rstd[:, own])
                else:
                    last = nc.vector.scalar_tensor_tensor(out=shift_n[:, own], in0=mv[:, own, 0], scalar=-1.0,
                                                          in1=rstd[:, own], op0=ALU.mult, op1=ALU.mult)
                last.then_inc(chain, 1)

            def low_part(high, nth, parts, t0, tiles, ready):
                dve.wait_ge(high, nth)
                nc.vector.scalar_tensor_tensor(out=parts[:, bass.ds(t0, tiles), D:2 * D],
                                               in0=xn[:, bass.ds(t0, tiles), :], scalar=HL,
                                               in1=parts[:, bass.ds(t0, tiles), 0:D],
                                               op0=ALU.mult, op1=ALU.subtract).then_inc(ready, 1)

            def finish(b, k):
                by_tile = att[:].rearrange("p h a i c -> p (h a i) c")
                if k == 0:
                    dve.wait_ge(back_taken, (b + 1) * HALVES)
                    nc.vector.reciprocal(rden[:], by_tile[:, :, F]).then_inc(att_chain, 1)
                elif k == 1:
                    dve.wait_ge(att_chain, b * ATT + 1)
                    nc.vector.tensor_tensor(by_tile[:, :, 0:F], by_tile[:, :, 0:F],
                                            rden[:].unsqueeze(2).broadcast_to([P, HEADS * BT, F]),
                                            ALU.mult).then_inc(att_chain, 1)
                elif k == 2:
                    dve.wait_ge(att_chain, b * ATT + 2)
                    for h in range(HEADS):
                        nodes = xn[:, bass.ds(b * BT, BT), h * F:(h + 1) * F]
                        last = nc.vector.tensor_tensor(nodes, nodes, by_tile[:, h * BT:(h + 1) * BT, 0:F], ALU.add)
                    last.then_inc(att_chain, 1)
                else:
                    if k == 3:
                        dve.wait_ge(att_chain, b * ATT + 3)
                    norm_step(att_chain, b * ATT + 3, b * BT, BT, k - 3)

            def finish_low(b):
                low_part(att_high, b + 1, parts_a, b * BT, BT, parts1_ready)

            def unit_block(b, first, final):
                for u in range(NT):
                    if u + 1 < NT:
                        scores(b, u + 1)
                    elif not final:
                        scores(b + 1, 0)
                    step = 2 * (u - FINISH_AT)
                    if not first and 0 <= step < ATT:
                        finish(b - 1, step)
                    weights(b, u)
                    if not first and 0 <= step < ATT - 1:
                        finish(b - 1, step + 1)
                    if not first and u == LOW_AT:
                        finish_low(b - 1)

            scores(0, 0)
            unit_block(0, True, False)
            with dve.Fori(1, NB - 1) as b:
                unit_block(b, False, False)
            unit_block(NB - 1, False, True)
            for k in range(ATT):
                finish(NB - 1, k)
            finish_low(NB - 1)
            dve.wait_ge(w23_loaded, 48)
            nc.vector.tensor_tensor(w3s[:, 0, :], w3s[:, 0, :], w3s[:, 1, :], ALU.add).then_inc(w3_ready, 1)

            def hyper(c, slot):
                link = linker(l1_chain, c * HYPER)
                dve.wait_ge(l1_summed, c + 1)
                dve.wait_ge(l1_low, c + 1)
                banks = ps[:, 4 * slot:4 * slot + 4, :]
                nc.vector.tensor_tensor(msg[:, slot, :, :], tmp[:, slot, :, :], banks[:, :, 0:D], ALU.add)
                link(nc.vector.tensor_scalar(deg[:, 0, :], banks[:, :, 2 * D], 0.0, None, ALU.is_equal))
                nc.vector.tensor_tensor(deg[:, 1, :], deg[:, 0, :], banks[:, :, 2 * D], ALU.add).then_inc(l1_taken, 1)
                dve.wait_ge(l1_taken, c + 1)
                link(nc.vector.tensor_scalar(deg[:, 2, :], deg[:, 0, :], -1.0 / HL, 1.0 / HL, ALU.mult, ALU.add))
                link(nc.vector.reciprocal(deg[:, 3, :], deg[:, 1, :]))
                link(nc.vector.tensor_tensor(deg[:, 3, :], deg[:, 3, :], deg[:, 2, :], ALU.mult))
                for i in range(GT):
                    node = xn[:, bass.ds(c * GT + i, 1), :].rearrange("p a d -> p (a d)")
                    last = nc.vector.scalar_tensor_tensor(out=node, in0=msg[:, slot, i, :],
                                                          scalar=deg[:, 3, i:i + 1], in1=node,
                                                          op0=ALU.mult, op1=ALU.add)
                link(last)
                for k in range(NORM):
                    norm_step(l1_chain, c * HYPER + 5, c * GT, GT, k)
                low_part(l1_high, c + 1, parts_b, c * GT, GT, parts2_ready)

            hyper(0, 0)
            hyper(1, 1)
            with dve.Fori(1, NG // 2) as i:
                hyper(2 * i, 0)
                hyper(2 * i + 1, 1)

            def aggregate(s, c, slot):
                dve.wait_ge(s["product"], c + 1)
                if s is agg[1]:
                    relu = act3[:, bass.ds(c * GT, GT), :].rearrange("p t d -> p (t d)")
                    nc.vector.tensor_scalar(relu, ps[:, 4 + slot, :], 0.0, None, ALU.max).then_inc(s["taken"], 1)
                    dve.wait_ge(s["taken"], c + 1)
                    if isinstance(c, int) and c == 0:
                        nc.vector.tensor_copy(relu_sum, relu).then_inc(s["chain"], 1)
                    else:
                        dve.wait_ge(s["chain"], c)
                        nc.vector.tensor_tensor(relu_sum, relu_sum, relu, ALU.add).then_inc(s["chain"], 1)
                    return
                tiles = xn[:, bass.ds(c * GT, GT), :].rearrange("p t d -> p (t d)")
                nc.vector.tensor_tensor(tiles, tiles, ps[:, 4 + slot, :], ALU.add).then_inc(s["taken"], 1)
                dve.wait_ge(s["taken"], c + 1)
                for k in range(NORM):
                    norm_step(s["chain"], c * NORM, c * GT, GT, k)
                low_part(s["high"], c + 1, parts_a, c * GT, GT, s["parts_out"])

            for s in agg:
                aggregate(s, 0, 0)
                aggregate(s, 1, 1)
                with dve.Fori(1, NG // 2) as i:
                    aggregate(s, 2 * i, 0)
                    aggregate(s, 2 * i + 1, 1)

            dve.wait_ge(colsum, 1)
            link = linker(end_chain, 0)
            link(nc.vector.tensor_scalar(mean_c, ps[:, 6, 0:D], 1.0 / N, None, ALU.mult))
            for i in range(NG):
                tiles = act3[:, i * GT:(i + 1) * GT, :]
                nc.vector.tensor_tensor(tiles, tiles, mean_c.unsqueeze(1).broadcast_to([P, GT, D]),
                                        ALU.subtract).then_inc(mean_copied, 1)
            dve.wait_ge(total_made, 1)
            link(nc.vector.reduce_sum(pn[:, 0:1], ps[:, 7, 0:NG], AX.X))
            link(nc.vector.tensor_scalar(pn[:, 1:2], pn[:, 0:1], 1.0 / N, PAIR_EPS, ALU.mult, ALU.add))
            for k in range(2 + 3 * NEWTON):
                link(rsqrt(k, pn[:, 1:2], pn[:, 2:3], pn[:, 3:4]))
            def count(ins):
                done[0] += 1
                ins.then_inc(end_chain, 1)
                return done[0]

            def residual(i):
                tiles = xn[:, i * GT:(i + 1) * GT, :]
                return nc.vector.scalar_tensor_tensor(out=tiles, in0=act3[:, i * GT:(i + 1) * GT, :],
                                                      scalar=pn[:, 3:4], in1=tiles, op0=ALU.mult, op1=ALU.add)

            def root(part, k, before):
                own = slice(END_PARTS[part][0] * GT, END_PARTS[part][1] * GT)
                dve.wait_ge(end_chain, before)
                if k == 0:
                    return count(nc.vector.tensor_scalar(var_all[:, 0, own], mv_all[:, own, 1], EPS, None, ALU.add))
                if k < ROOT - 1:
                    return count(rsqrt(k - 1, var_all[:, 0, own], var_all[:, 1, own], rstd_all[:, own]))
                return nc.vector.scalar_tensor_tensor(out=shift_all[:, own], in0=mv_all[:, own, 0], scalar=-1.0,
                                                      in1=rstd_all[:, own], op0=ALU.mult, op1=ALU.mult
                                                      ).then_inc(stats_ready, 1)

            done = [2 + 2 + 2 + 3 * NEWTON - 1]
            for part, (start, stop) in enumerate(END_PARTS):
                k = 0 if part else ROOT
                moved = count(residual(start))
                for i in range(start, stop):
                    arrived = moved
                    if i + 1 < stop:
                        moved = count(residual(i + 1))
                    for t in range(i * GT, (i + 1) * GT):
                        if k < ROOT:
                            rooted = root(part - 1, k, rooted)
                            k += 1
                        if t == i * GT:
                            dve.wait_ge(end_chain, arrived)
                        last = nc.vector.bn_stats(st_all[:, t, :], xn[:, t, :])
                    measured = count(last)
                while k < ROOT:
                    rooted = root(part - 1, k, rooted)
                    k += 1
                dve.wait_ge(end_chain, measured)
                for t in range(start * GT, stop * GT):
                    last = nc.vector.bn_aggr(mv_all[:, t, :], st_all[:, t, :])
                rooted = count(last)
            for k in range(ROOT):
                rooted = root(len(END_PARTS) - 1, k, rooted)
            dve.wait_ge(stats_ready, len(END_PARTS))
            for i in VECTOR_CHUNKS:
                for t in range(i * GT, (i + 1) * GT):
                    last = nc.vector.tensor_scalar(xn[:, t, :], xn[:, t, :], mv_all[:, t, 0:1], rstd_all[:, t:t + 1],
                                                   ALU.subtract, ALU.mult)
                last.then_inc(out_ready[0], 1)


_INS = ['x', 'adj', 'L0_gnn_kernels', 'L0_gnn_att_kernels', 'L2_gnn_weight', 'L3_gnn_weight', 'L3_gnn_self_weight']


def kernel(**inputs):
    import numpy as _np
    import concourse.bacc as _bacc
    from concourse import mybir as _mybir
    from concourse.bass_utils import run_bass_kernel_spmd as _run

    nc = _bacc.Bacc("TRN2", target_bir_lowering=False, num_devices=1)
    arrays, args = {}, []
    for name in _INS:
        a = _np.ascontiguousarray(inputs[name])
        arrays[f"in_{name}"] = a
        args.append(nc.dram_tensor(f"in_{name}", a.shape, _mybir.dt.from_np(a.dtype), kind="ExternalInput").ap())
    args.append(nc.dram_tensor("out_0", inputs["x"].shape, _mybir.dt.float32, kind="ExternalOutput").ap())
    build(nc, *args)
    r = _run(nc, [arrays], core_ids=[0])
    return r.results[0]["out_0"]
```
